# Optimizing a Trainium2 kernel written in Bass

```python
import numpy as np
import jax
import jax.numpy as jnp

def _softmax(x, axis=-1):
    return jax.nn.softmax(x, axis=axis)

def _gelu(x):
    return jax.nn.gelu(x, approximate=True)

def _silu(x):
    return jax.nn.silu(x)

def _sigmoid(x):
    return jax.nn.sigmoid(x)

def _layernorm(x, axis=-1, eps=1e-05):
    m = jnp.mean(x, axis=axis, keepdims=True)
    v = jnp.var(x, axis=axis, keepdims=True)
    return (x - m) / jnp.sqrt(v + eps)

def _scatter_add(tgt, idx, src, axis=0):
    return tgt.at[idx].add(src)

def _segment_sum(src, seg, n):
    return jax.ops.segment_sum(src, seg, n)
kernel_name = 'mk_flamingo_gated_d2_seqx_r8_933bc5'

def setup_inputs(seed: int=0):
    np.random.seed(seed)
    _w = jnp.asarray

    def _rec_inputs():
        import jax
        import jax.numpy as jnp
        _rk = jax.random.key(seed)
        x = 2.818e-05 + 1 * jax.random.normal(jax.random.fold_in(_rk, 1), (4, 256, 128), jnp.float32)
        _lenS = 256 - jax.random.randint(jax.random.fold_in(_rk, 7), (4,), 0, max(1, 256 // 4) + 1, jnp.int32)
        _lenS2 = 256 - jax.random.randint(jax.random.fold_in(_rk, 8), (4,), 0, max(1, 256 // 4) + 1, jnp.int32)
        _ctx_2048P = jax.random.normal(jax.random.fold_in(_rk, 11), (4, 16, 256), jnp.float32)
        _ctx_2048c = jax.random.dirichlet(jax.random.fold_in(_rk, 511), 0.3 * jnp.ones((16,), jnp.float32), (4, 256))
        _ctx_2048t = jnp.einsum('bsk,bkd->bsd', _ctx_2048c, _ctx_2048P)
        _ctx_2048t = _ctx_2048t * jax.lax.rsqrt(jnp.mean(jnp.square(_ctx_2048t)) + 1e-12) * 0.953939
        ctx_2048 = -0.000125008 + 0.999885 * (_ctx_2048t + 0.3 * jax.random.normal(jax.random.fold_in(_rk, 611), (4, 256, 256), jnp.float32))
        _validS = jnp.arange(256)[None, :] < _lenS[:, None]
        _validS2 = jnp.arange(256)[None, :] < _lenS2[:, None]
        _causal = jnp.tril(jnp.ones((256, 256), dtype=bool))
        mask_BxS2_fk1 = jnp.where(jnp.broadcast_to(_validS2[:, :], (4, 256)), 1.0, 0.0).astype(jnp.float32)
        mask_BxS2_if0 = jnp.where(jnp.ones((4, 256), dtype=bool), 4, 0).astype(jnp.int32)
        _g = jax.random.normal(jax.random.fold_in(_rk, 9001), (2, 2), jnp.float32)
        _g = jnp.sign(_g) * jnp.maximum(jnp.abs(_g), 1.0) + (_g == 0) * 1.0
        g_xattn = _g[0]
        g_ffn = _g[1]
        return (x, ctx_2048, mask_BxS2_fk1, mask_BxS2_if0, g_xattn, g_ffn)
    x, ctx_2048, mask_BxS2_fk1, mask_BxS2_if0, g_xattn, g_ffn = _rec_inputs()

    def _L0_xattn_setup():
        import jax, jax.numpy as jnp
        import numpy as np
        B, S, T = (32, 64, 64)
        SRC_SIZE, TGT_SIZE, OUT_SIZE, NUM_HEAD = (256, 128, 128, 8)
        HEAD_DIM = OUT_SIZE // NUM_HEAD
        key = jax.random.key(seed)
        ks = jax.random.split(key, 12)
        src = jax.random.normal(ks[0], (B, S, SRC_SIZE), dtype=jnp.float32)
        tgt = jax.random.normal(ks[1], (B, T, TGT_SIZE), dtype=jnp.float32)
        src_mask = (jax.random.uniform(ks[2], (B, S)) > 0.3).astype(jnp.float32)
        src_mask = src_mask.at[:, 0].set(1.0)
        tgt_mask = (jax.random.uniform(ks[3], (B, T)) > 0.3).astype(jnp.float32)
        tgt_mask = tgt_mask.at[:, 0].set(1.0)

        def lin(k, out_f, in_f):
            return jax.random.normal(k, (out_f, in_f), dtype=jnp.float32) / np.sqrt(in_f)
        W_src = lin(ks[4], 2 * OUT_SIZE, SRC_SIZE)
        b_src = jnp.zeros((2 * OUT_SIZE,), jnp.float32)
        W_tgt = lin(ks[5], OUT_SIZE, TGT_SIZE)
        b_tgt = jnp.zeros((OUT_SIZE,), jnp.float32)
        W_out = lin(ks[6], OUT_SIZE, OUT_SIZE + TGT_SIZE)
        b_out = jnp.zeros((OUT_SIZE,), jnp.float32)
        return {'src': src, 'tgt': tgt, 'src_mask': src_mask, 'tgt_mask': tgt_mask, 'W_src': W_src, 'b_src': b_src, 'W_tgt': W_tgt, 'b_tgt': b_tgt, 'W_out': W_out, 'b_out': b_out}
    _L0_xattn_all = _L0_xattn_setup()
    _L0_xattn_in = {k: v for k, v in _L0_xattn_all.items() if k in ('W_src', 'b_src', 'W_tgt', 'b_tgt', 'W_out', 'b_out')}
    del _L0_xattn_all

    def _L0_ffn_setup():
        import jax, jax.numpy as jnp
        import numpy as np
        N_HEAD = 16
        N_ACTIVE = 4
        D_MODEL = 128
        D_ATTN = 64
        B = 4
        S = 256
        key = jax.random.key(seed)
        ks = jax.random.split(key, 6)
        sc = 1.0 / np.sqrt(D_MODEL).astype(np.float32)
        return {'x': jax.random.normal(ks[0], (B, S, D_MODEL), jnp.float32), 'Wq': jax.random.normal(ks[1], (D_MODEL, N_HEAD * D_ATTN), jnp.float32) * sc, 'bq': jnp.zeros((N_HEAD * D_ATTN,), jnp.float32), 'Wk': jax.random.normal(ks[2], (D_MODEL, N_HEAD * D_ATTN), jnp.float32) * sc, 'bk': jnp.zeros((N_HEAD * D_ATTN,), jnp.float32), 'Wv': jax.random.normal(ks[3], (D_MODEL, N_HEAD * D_ATTN), jnp.float32) * sc, 'bv': jnp.zeros((N_HEAD * D_ATTN,), jnp.float32), 'Wr': jax.random.normal(ks[4], (D_MODEL, N_HEAD), jnp.float32) * sc, 'br': jnp.zeros((N_HEAD,), jnp.float32), 'Wo': jax.random.normal(ks[5], (N_ACTIVE * D_ATTN, D_MODEL), jnp.float32) * (1.0 / np.sqrt(N_ACTIVE * D_ATTN).astype(np.float32)), 'bo': jnp.zeros((D_MODEL,), jnp.float32)}
    _L0_ffn_all = _L0_ffn_setup()
    _L0_ffn_in = {k: v for k, v in _L0_ffn_all.items() if k in ('Wq', 'bq', 'Wk', 'bk', 'Wv', 'bv', 'Wr', 'br', 'Wo', 'bo')}
    del _L0_ffn_all

    def _L1_xattn_setup():
        import jax, jax.numpy as jnp
        import numpy as np
        B, L, P = (4, 512, 128)
        D_MODEL = 128
        D_GLOBAL = 256
        HEADDIM = 32
        EPSILON = 0.001
        RMS_EPS = 1e-05

        def rmsnorm(x, g, eps=RMS_EPS):
            var = jnp.mean(jnp.square(x), axis=-1, keepdims=True)
            return x * jax.lax.rsqrt(var + eps) * g

        def _hnet_depool(h, h_patch_full, patch_lens):
            h_patch = h_patch_full[..., :D_MODEL]
            bsz, plen = (h_patch.shape[0], h_patch.shape[1])
            seqlen = h.shape[1]
            logp = jnp.full((bsz, plen), -EPSILON, dtype=jnp.float32)
            bidx = jnp.cumsum(patch_lens, axis=1) - 1
            boundary_mask = jnp.zeros((bsz, seqlen), dtype=jnp.int32)
            boundary_mask = boundary_mask.at[jnp.arange(bsz)[:, None], bidx].set(1)
            dt = (-jnp.log(-jnp.expm1(logp))).astype(h_patch.dtype)
            x = h_patch / dt[..., None]
            n_heads = D_MODEL // HEADDIM
            A = -jnp.ones((n_heads,), dtype=jnp.float32)
            bcoef = jnp.exp(logp).astype(h_patch.dtype)
            x4 = x.reshape(bsz, plen, n_heads, HEADDIM)
            a = jnp.exp(dt[:, :, None] * A[None, None, :])
            u = (dt * bcoef)[:, :, None, None] * x4
            a_b = jnp.broadcast_to(a[..., None], u.shape)

            def comb(lft, rgt):
                aL, uL = lft
                aR, uR = rgt
                return (aL * aR, uL * aR + uR)
            _, s = jax.lax.associative_scan(comb, (a_b, u), axis=1)
            depool = s.reshape(bsz, plen, D_MODEL)
            plug = jnp.clip(jnp.cumsum(boundary_mask, axis=1) - 1, 0, plen - 1)
            depool_out = depool[jnp.arange(bsz)[:, None], plug]
            return depool_out + h
        key = jax.random.key(seed)
        k1, k2, k3, k4 = jax.random.split(key, 4)
        embeds = jax.random.normal(k1, (B, L, D_MODEL), dtype=jnp.float32)
        patch_embeds = jax.random.normal(k2, (B, P, D_GLOBAL), dtype=jnp.float32)
        patch_lens = jnp.full((B, P), L // P, dtype=jnp.int64)
        W_in = jax.random.normal(k3, (D_MODEL, D_MODEL), dtype=jnp.float32) * 0.02
        b_in = jnp.zeros((D_MODEL,), dtype=jnp.float32)
        g_res = jnp.ones((D_MODEL,), dtype=jnp.float32)
        g_init = jnp.ones((D_GLOBAL,), dtype=jnp.float32)
        return {'embeds': embeds, 'patch_embeds': patch_embeds, 'patch_lens': patch_lens, 'W_in': W_in, 'b_in': b_in, 'g_res': g_res, 'g_init': g_init}
    _L1_xattn_all = _L1_xattn_setup()
    _L1_xattn_in = {k: v for k, v in _L1_xattn_all.items() if k in ('W_in', 'b_in', 'g_res', 'g_init')}
    del _L1_xattn_all

    def _L1_ffn_setup():
        import jax, jax.numpy as jnp
        import numpy as np
        D = 128
        H = 128
        E = 8
        K = 2
        I = 2 * 128
        ROUTE_SCALE = 1.0
        key = jax.random.key(seed)
        ks = jax.random.split(key, 12)
        s = lambda *sh: 1.0 / np.sqrt(sh[-1])
        return {'x': jax.random.normal(ks[0], (1, 256, D), jnp.float32), 'gate_w': jax.random.normal(ks[1], (E, D), jnp.float32) * s(E, D), 'w1': jax.random.normal(ks[2], (E, H, D), jnp.float32) * s(H, D), 'b1': jax.random.normal(ks[3], (E, H), jnp.float32) * 0.01, 'w2': jax.random.normal(ks[4], (E, D, H), jnp.float32) * s(D, H), 'b2': jax.random.normal(ks[5], (E, D), jnp.float32) * 0.01, 'w3': jax.random.normal(ks[6], (E, H, D), jnp.float32) * s(H, D), 'b3': jax.random.normal(ks[7], (E, H), jnp.float32) * 0.01, 'sw1': jax.random.normal(ks[8], (I, D), jnp.float32) * s(I, D), 'sw2': jax.random.normal(ks[9], (I, D), jnp.float32) * s(I, D), 'sw3': jax.random.normal(ks[10], (D, I), jnp.float32) * s(D, I)}
    _L1_ffn_all = _L1_ffn_setup()
    _L1_ffn_in = {k: v for k, v in _L1_ffn_all.items() if k in ('gate_w', 'w1', 'b1', 'w2', 'b2', 'w3', 'b3', 'sw1', 'sw2', 'sw3')}
    del _L1_ffn_all
    return {'x': x, 'ctx_2048': ctx_2048, 'mask_BxS2_fk1': mask_BxS2_fk1, 'mask_BxS2_if0': mask_BxS2_if0, 'g_xattn': g_xattn, 'g_ffn': g_ffn, 'L0_xattn_W_src': _L0_xattn_in['W_src'], 'L0_xattn_b_src': _L0_xattn_in['b_src'], 'L0_xattn_W_tgt': _L0_xattn_in['W_tgt'], 'L0_xattn_b_tgt': _L0_xattn_in['b_tgt'], 'L0_xattn_W_out': _L0_xattn_in['W_out'], 'L0_xattn_b_out': _L0_xattn_in['b_out'], 'L0_ffn_Wq': _L0_ffn_in['Wq'], 'L0_ffn_bq': _L0_ffn_in['bq'], 'L0_ffn_Wk': _L0_ffn_in['Wk'], 'L0_ffn_bk': _L0_ffn_in['bk'], 'L0_ffn_Wv': _L0_ffn_in['Wv'], 'L0_ffn_bv': _L0_ffn_in['bv'], 'L0_ffn_Wr': _L0_ffn_in['Wr'], 'L0_ffn_br': _L0_ffn_in['br'], 'L0_ffn_Wo': _L0_ffn_in['Wo'], 'L0_ffn_bo': _L0_ffn_in['bo'], 'L1_xattn_W_in': _L1_xattn_in['W_in'], 'L1_xattn_b_in': _L1_xattn_in['b_in'], 'L1_xattn_g_res': _L1_xattn_in['g_res'], 'L1_xattn_g_init': _L1_xattn_in['g_init'], 'L1_ffn_gate_w': _L1_ffn_in['gate_w'], 'L1_ffn_w1': _L1_ffn_in['w1'], 'L1_ffn_b1': _L1_ffn_in['b1'], 'L1_ffn_w2': _L1_ffn_in['w2'], 'L1_ffn_b2': _L1_ffn_in['b2'], 'L1_ffn_w3': _L1_ffn_in['w3'], 'L1_ffn_b3': _L1_ffn_in['b3'], 'L1_ffn_sw1': _L1_ffn_in['sw1'], 'L1_ffn_sw2': _L1_ffn_in['sw2'], 'L1_ffn_sw3': _L1_ffn_in['sw3']}

def reference(x, ctx_2048, mask_BxS2_fk1, mask_BxS2_if0, g_xattn, g_ffn, L0_xattn_W_src, L0_xattn_b_src, L0_xattn_W_tgt, L0_xattn_b_tgt, L0_xattn_W_out, L0_xattn_b_out, L0_ffn_Wq, L0_ffn_bq, L0_ffn_Wk, L0_ffn_bk, L0_ffn_Wv, L0_ffn_bv, L0_ffn_Wr, L0_ffn_br, L0_ffn_Wo, L0_ffn_bo, L1_xattn_W_in, L1_xattn_b_in, L1_xattn_g_res, L1_xattn_g_init, L1_ffn_gate_w, L1_ffn_w1, L1_ffn_b1, L1_ffn_w2, L1_ffn_b2, L1_ffn_w3, L1_ffn_b3, L1_ffn_sw1, L1_ffn_sw2, L1_ffn_sw3):
    import jax
    import jax.numpy as jnp

    def _L0_xattn_ref(src, tgt, src_mask, tgt_mask, W_src, b_src, W_tgt, b_tgt, W_out, b_out):
        import jax, jax.numpy as jnp
        import numpy as np
        B, S, T = (32, 64, 64)
        SRC_SIZE, TGT_SIZE, OUT_SIZE, NUM_HEAD = (256, 128, 128, 8)
        HEAD_DIM = OUT_SIZE // NUM_HEAD
        b, s, _ = src.shape
        t = tgt.shape[1]
        src_trans = jnp.einsum('bsf,of->bso', src, W_src) + b_src
        tgt_trans = jnp.einsum('btf,of->bto', tgt, W_tgt) + b_tgt
        src_trans = src_trans * src_mask[:, :, None]
        tgt_trans = tgt_trans * tgt_mask[:, :, None]
        src_key, src_val = jnp.split(src_trans, 2, axis=2)
        k = src_key.reshape(b, s, NUM_HEAD, HEAD_DIM)
        v = src_val.reshape(b, s, NUM_HEAD, HEAD_DIM)
        q = tgt_trans.reshape(b, t, NUM_HEAD, HEAD_DIM)
        scores = jnp.einsum('bthd,bshd->bhts', q, k) / np.sqrt(HEAD_DIM)
        scores = jnp.where(src_mask[:, None, None, :] == 0, -jnp.inf, scores)
        attn = jax.nn.softmax(scores, axis=-1)
        tgt_update = jnp.einsum('bhts,bshd->bthd', attn, v).reshape(b, t, OUT_SIZE)
        cat_tgt = jnp.concatenate([tgt, tgt_update], axis=2)
        return jnp.einsum('btf,of->bto', cat_tgt, W_out) + b_out

    def _L0_ffn_ref(x, Wq, bq, Wk, bk, Wv, bv, Wr, br, Wo, bo):
        import jax, jax.numpy as jnp
        import numpy as np
        N_HEAD = 16
        N_ACTIVE = 4
        D_MODEL = 128
        D_ATTN = 64
        B = 4
        S = 256
        b, s, _ = x.shape
        dist = jax.nn.softmax(jnp.mean(x @ Wr + br, axis=1), axis=-1)
        _, idx = jax.lax.top_k(dist, N_ACTIVE)
        idx = jnp.sort(idx, axis=-1)

        def proj(W, bias):
            return (x @ W + bias).reshape(b, s, N_HEAD, D_ATTN).transpose(0, 2, 1, 3)
        Q = proj(Wq, bq)
        K = proj(Wk, bk)
        V = proj(Wv, bv)
        gather = lambda t: jnp.take_along_axis(t, idx[:, :, None, None], axis=1)
        Qs, Ks, Vs = (gather(Q), gather(K), gather(V))
        scale = 1.0 / jnp.sqrt(jnp.asarray(D_ATTN, x.dtype))
        score = jax.nn.softmax(jnp.einsum('bhqd,bhkd->bhqk', Qs, Ks) * scale, axis=-1)
        O = jnp.einsum('bhqk,bhkd->bhqd', score, Vs)
        O = O.transpose(0, 2, 1, 3).reshape(b, s, N_ACTIVE * D_ATTN)
        return O @ Wo + bo

    def _L1_xattn_ref(embeds, patch_embeds, patch_lens, W_in, b_in, g_res, g_init):
        import jax, jax.numpy as jnp
        import numpy as np
        B, L, P = (4, 512, 128)
        D_MODEL = 128
        D_GLOBAL = 256
        HEADDIM = 32
        EPSILON = 0.001
        RMS_EPS = 1e-05

        def rmsnorm(x, g, eps=RMS_EPS):
            var = jnp.mean(jnp.square(x), axis=-1, keepdims=True)
            return x * jax.lax.rsqrt(var + eps) * g

        def _hnet_depool(h, h_patch_full, patch_lens):
            h_patch = h_patch_full[..., :D_MODEL]
            bsz, plen = (h_patch.shape[0], h_patch.shape[1])
            seqlen = h.shape[1]
            logp = jnp.full((bsz, plen), -EPSILON, dtype=jnp.float32)
            bidx = jnp.cumsum(patch_lens, axis=1) - 1
            boundary_mask = jnp.zeros((bsz, seqlen), dtype=jnp.int32)
            boundary_mask = boundary_mask.at[jnp.arange(bsz)[:, None], bidx].set(1)
            dt = (-jnp.log(-jnp.expm1(logp))).astype(h_patch.dtype)
            x = h_patch / dt[..., None]
            n_heads = D_MODEL // HEADDIM
            A = -jnp.ones((n_heads,), dtype=jnp.float32)
            bcoef = jnp.exp(logp).astype(h_patch.dtype)
            x4 = x.reshape(bsz, plen, n_heads, HEADDIM)
            a = jnp.exp(dt[:, :, None] * A[None, None, :])
            u = (dt * bcoef)[:, :, None, None] * x4
            a_b = jnp.broadcast_to(a[..., None], u.shape)

            def comb(lft, rgt):
                aL, uL = lft
                aR, uR = rgt
                return (aL * aR, uL * aR + uR)
            _, s = jax.lax.associative_scan(comb, (a_b, u), axis=1)
            depool = s.reshape(bsz, plen, D_MODEL)
            plug = jnp.clip(jnp.cumsum(boundary_mask, axis=1) - 1, 0, plen - 1)
            depool_out = depool[jnp.arange(bsz)[:, None], plug]
            return depool_out + h
        h = rmsnorm(embeds, g_res)
        h = jnp.einsum('bld,ed->ble', h, W_in) + b_in
        h_patch = rmsnorm(patch_embeds, g_init)
        return _hnet_depool(h, h_patch, patch_lens)

    def _L1_ffn_ref(x, gate_w, w1, b1, w2, b2, w3, b3, sw1, sw2, sw3):
        import jax, jax.numpy as jnp
        import numpy as np
        D = 128
        H = 128
        E = 8
        K = 2
        I = 2 * 128
        ROUTE_SCALE = 1.0
        B, S, _ = x.shape
        xt = x.reshape(-1, D)
        logits = xt @ gate_w.T
        scores = jax.nn.softmax(logits.astype(jnp.float32), axis=-1)
        top_vals, idx = jax.lax.top_k(scores, K)
        weights = jnp.take_along_axis(scores, idx, axis=1).astype(x.dtype) * ROUTE_SCALE
        xs = xt[:, None, :] * weights[:, :, None]
        y = jnp.zeros_like(xt)
        for e in range(E):
            mask = (idx == e).astype(x.dtype)
            h = jax.nn.silu(jnp.einsum('tkd,hd->tkh', xs, w1[e]) + b1[e])
            x2 = jnp.einsum('tkh,dh->tkd', h, w2[e]) + b2[e]
            x3 = jnp.einsum('tkd,hd->tkh', xs, w3[e]) + b3[e]
            y = y + jnp.sum(x2 * x3 * mask[:, :, None], axis=1)
        z = jax.nn.silu(xt @ sw1.T) * (xt @ sw2.T) @ sw3.T
        return (y + z).reshape(B, S, D)
    x = x + jnp.tanh(g_xattn[0]) * _L0_xattn_ref(ctx_2048, _layernorm(x, axis=-1), mask_BxS2_fk1, mask_BxS2_fk1, L0_xattn_W_src, L0_xattn_b_src, L0_xattn_W_tgt, L0_xattn_b_tgt, L0_xattn_W_out, L0_xattn_b_out)
    x = x + jnp.tanh(g_ffn[0]) * _L0_ffn_ref(_layernorm(x, axis=-1), L0_ffn_Wq, L0_ffn_bq, L0_ffn_Wk, L0_ffn_bk, L0_ffn_Wv, L0_ffn_bv, L0_ffn_Wr, L0_ffn_br, L0_ffn_Wo, L0_ffn_bo)
    x = x + jnp.tanh(g_xattn[1]) * _L1_xattn_ref(_layernorm(x, axis=-1), ctx_2048, mask_BxS2_if0, L1_xattn_W_in, L1_xattn_b_in, L1_xattn_g_res, L1_xattn_g_init)
    x = x + jnp.tanh(g_ffn[1]) * _L1_ffn_ref(_layernorm(x, axis=-1), L1_ffn_gate_w, L1_ffn_w1, L1_ffn_b1, L1_ffn_w2, L1_ffn_b2, L1_ffn_w3, L1_ffn_b3, L1_ffn_sw1, L1_ffn_sw2, L1_ffn_sw3)
    return x

_drawn_inputs = setup_inputs


def setup_inputs(seed=0):
    import zlib

    import numpy as np

    out = dict(_drawn_inputs(seed))
    spreads = {'g_ffn': (-1.0, 0.6),
     'L0_xattn_b_src': (0.0, 0.1),
     'L0_xattn_b_tgt': (0.0, 0.8),
     'L0_xattn_b_out': (0.0, 0.1),
     'L0_ffn_bq': (0.0, 0.8),
     'L0_ffn_bk': (0.0, 2.0),
     'L0_ffn_bv': (0.0, 0.1),
     'L0_ffn_br': (0.0, 0.1),
     'L0_ffn_bo': (0.0, 0.1),
     'L1_xattn_b_in': (0.0, 0.1),
     'L1_xattn_g_res': (1.0, 0.568),
     'L1_xattn_g_init': (1.0, 0.2)}
    factors = {'L1_ffn_b1': 45.15, 'L1_ffn_b2': 21.334, 'L1_ffn_b3': 39.06}
    for name, (base, spread) in spreads.items():
        noise = np.random.default_rng([zlib.crc32(name.encode()), seed]).standard_normal(out[name].shape)
        drawn = base * np.exp(spread * noise) if base else spread * noise
        out[name] = jnp.asarray(drawn.astype(out[name].dtype))
    for name, factor in factors.items():
        out[name] = (out[name] * factor).astype(out[name].dtype)
    return out
```

```python
from contextlib import ExitStack

import concourse.bass as bass
from concourse import mybir

F32 = mybir.dt.float32
F32R = mybir.dt.float32r
BF16 = mybir.dt.bfloat16
I32 = mybir.dt.int32
U32 = mybir.dt.uint32
ALU = mybir.AluOpType
ACT = mybir.ActivationFunctionType
AX = mybir.AxisListType

P = 128
B = 4
T = 256
TT = T // P
D = 128
DC = 256
CC = DC // P
H1, HD1 = 8, 16
PAIRS = H1 // 2
NH, NA, HD2 = 16, 4, 64
E = 8
HALVES = 2
EPS = 1e-5
MASKED = -1e30
RING = 4

STACK = 3 * HD1
ROW_BIAS = STACK
ROW_MAX = STACK + 1

USES = {
    "plan_a": (0, 1), "plan_b": (0, 1), "plan_c": (0, 1), "u": (0, 0), "depool": (1, 0),
    "kv": (0, 2), "q": (0, 1),
    "stat": (0, 0), "norm": (1, 0),
    "s1": (0, 1), "max1": (1, 0), "st1": (1, 0), "pv1": (0, 1), "o1": (1, 0), "y1": (0, 1),
    "route": (0, 1), "qkv2": (3, 0), "s2": (1, 0), "pt2": (0, 1), "pv2": (0, 1), "o2": (1, 0), "y2": (0, 1),
    "y3": (0, 1),
    "gate": (0, 1), "gate_t": (1, 0), "wide": (0, 1), "up": (1, 0), "down": (0, 1),
    "shared": (1, 1), "y4": (0, 1),
}


def first_layer_front(b):
    return [("stat", b, 0), ("kv", b, 0), ("norm", b, 0), ("q", b, 0)]


def make_schedule():
    steps = first_layer_front(0)
    steps += [("plan_a", 0, 0), ("plan_b", 0, 0)]
    steps += first_layer_front(1)
    for slot in range(B + 2):
        a, b, c = slot, slot - 1, slot - 2
        has_a, has_b, has_c = a < B, 0 <= b < B, 0 <= c < B
        s1 = [("s1", a, h) for h in range(H1)] if has_a else []
        if has_c:
            steps += [("stat", c, 2)]
        if has_b:
            steps += [("stat", b, 1)]
        steps += s1[0:2]
        if has_b:
            steps += [("norm", b, 1), ("route", b, 0)]
        if has_c:
            steps += [("norm", c, 2), ("y3", c, 0), ("stat", c, 3)]
        steps += s1[2:4]
        if has_c:
            steps += [("norm", c, 3), ("gate", c, 0)]
        steps += s1[4:6]
        if has_c:
            steps += [("gate_t", c, 0), ("wide", c, 0)]
        steps += s1[6:8]
        if has_a:
            steps += [("max1", a, 0)]
        if has_c:
            for e in range(E):
                steps += [("wide", c, e + 1)] * (e + 1 < E) + [("up", c, e)] + [("down", c, e - 1)] * (e > 0)
            steps += [("shared", c, 0), ("down", c, E - 1), ("y4", c, 0)]
        if slot == 0:
            steps += [("u", 0, 0)]
        if slot < B:
            steps += [("depool", slot, 0)]
        if has_b:
            steps += [("plan_c", b, 0), ("qkv2", b, 0)]
        if 1 <= slot and slot + 1 < B:
            steps += first_layer_front(slot + 1)
        for h in range(H1):
            if has_a:
                steps += [("st1", a, h)]
            if has_b:
                if h % 2 == 0:
                    steps += [("s2", b, h // 2)]
                elif h >= 3:
                    steps += [("pt2", b, (h - 3) // 2)]
        if has_b:
            steps += [("pt2", b, NA - 1), ("pv2", b, 0)]
        if has_a:
            steps += [("pv1", a, 0)]
        if has_b:
            steps += [("o2", b, 0), ("y2", b, 0)]
        if has_a:
            steps += [("o1", a, 0), ("y1", a, 0)]
    return steps


SCHEDULE = make_schedule()
ACT_AT, DVE_AT = {}, {}
_act, _dve = 0, 0
for _step in SCHEDULE:
    assert _step not in ACT_AT
    ACT_AT[_step], DVE_AT[_step] = _act, _dve
    _act += USES[_step[0]][0]
    _dve += USES[_step[0]][1]


def order_of(name):
    return {step: n for n, step in enumerate(s for s in SCHEDULE if s[0] == name)}


STAT_AT, NORM_AT = order_of("stat"), order_of("norm")
NORMS = list(NORM_AT)
PARTS_AT = {step: n for n, step in enumerate(s for s in SCHEDULE if s[0] in ("kv", "q"))}
XN_BUFS = 4
EXPERT_BUFS = 3


def expert(k):
    return ("down", k // E, k % E)


def columns(*fields):
    at, out = 0, {}
    for name, width in fields:
        out[name] = (at, at + width)
        at += width
    return out, at


PACK_A, PACK_A_W = columns(("wk", CC * D), ("wv", CC * D), ("wq", D), ("bq", 1), ("bk", 1), ("bv", D),
                           ("mask_col", B * TT))
PACK_C, PACK_C_W = columns(("ident", P), ("tri", P), ("ones", P), ("decay", 3 * P), ("position", T),
                           ("row", 2), ("alpha", 1))
PACK_B, PACK_B_W = columns(("wo_x", D), ("wo_u", D), ("b_out", D), ("wr", NH), ("br", NH),
                           ("wo2", 2 * D), ("bo", D), ("w_in", D), ("b_in", D), ("g_res", 1), ("g_init", D),
                           ("gates", 4))
PACK_E, PACK_E_W = columns(("gate", E), ("b1", E), ("b2", E), ("sw1", HALVES * P), ("sw2", HALVES * P),
                           ("sw3", HALVES * D), ("w1", E * D), ("w3", E * D), ("w2", E * D))
GATE_ROWS = 4 * E


def flamingo(nc, x, ctx_tok, ctx_feat, pack_a, pack_b, pack_c, pack_e, mask_bc, mask_row, lens,
             head_w, head_b, sel_in, b3_in, out):
    with ExitStack() as stack:
        def sb(name, shape, dt=F32):
            return stack.enter_context(nc.sbuf_tensor(name, shape, dt))

        def sem(name):
            return stack.enter_context(nc.semaphore(name))

        xs = sb("xs", [P, B * TT, D])
        x1 = sb("x1", [P, 2 * TT, D])
        x2 = sb("x2", [P, 2 * TT, D])
        x3 = sb("x3", [P, 2 * TT, D])
        resid = [xs, x1, x2, x3]
        outs = xs
        ctok = sb("ctok", [P, B * TT, DC])
        cT = sb("cT", [P, B, CC, T])
        wa = sb("wa", [P, PACK_A_W])
        wb = sb("wb", [P, PACK_B_W])
        wc = sb("wc", [P, PACK_C_W])
        we = sb("we", [P, PACK_E_W])
        maskb = sb("maskb", [P, B, T])
        lens_i = sb("lens_i", [P, TT, B], I32)

        def A(name):
            return wa[:, PACK_A[name][0]:PACK_A[name][1]]

        def W(name):
            return wb[:, PACK_B[name][0]:PACK_B[name][1]]

        def C(name):
            return wc[:, PACK_C[name][0]:PACK_C[name][1]]

        def X(name):
            return we[:, PACK_E[name][0]:PACK_E[name][1]]

        ident = C("ident")

        tg = sb("tg", [P, 4])
        gated_bias = sb("gated_bias", [P, 3, D])
        base = [sb(f"base{k}", [P, 2, TT, D]) for k in range(3)]
        w_in_g = sb("w_in_g", [P, D])
        half = sb("half", [P, TT])
        bias_row = sb("bias_row", [1, B, T], F32R)
        sel = sb("sel", [GATE_ROWS, E, P], F32R)
        b3s = sb("b3s", [GATE_ROWS, E, P], F32R)

        lens_f = sb("lens_f", [P, TT, B])
        bidx = sb("bidx", [P, TT, B])
        wrapped = sb("wrapped", [P, TT, B])
        p2 = sb("p2", [P, NA, TT, T])
        hits = p2
        pT2 = sb("pT2", [P, NA, TT, T])
        sel_f = pT2[0:GATE_ROWS, 0:2].rearrange("p a c t -> p (a c t)")
        b3_f = pT2[0:GATE_ROWS, 2:4].rearrange("p a c t -> p (a c t)")
        b3_hi = p2[0:GATE_ROWS, 0:2].rearrange("p a c t -> p (a c t)").bitcast(F32R)
        bound = sb("bound", [P, TT, B])
        pick = sb("pick", [P, 2, TT, T])
        ssq = sb("ssq", [P, B * TT])
        sq_junk = sb("sq_junk", [P, 2, DC])
        const_rows = sb("const_rows", [1, 2, T], F32R)
        ms = sb("ms", [P, B * TT])
        rs = sb("rs", [P, B * TT])
        half8 = sb("half8", [P, B * TT])
        u = sb("u", [P, B * TT, D])
        dp = sb("dp", [P, B, TT, D])

        st = sb("st", [P, B, 4, TT, 6])
        mv = sb("mv", [P, B, 4, TT, 2])
        veps = sb("veps", [P, B, 4, TT])
        rstd = sb("rstd", [P, B, 4, TT])
        xn = sb("xn", [P, XN_BUFS, TT, D])
        xnT = [sb(f"xnT{k}", [P, 2, T]) for k in range(4)]
        xsum = sb("xsum", [P, B])

        qkf = sb("qkf", [P, 2, T])
        parts = sb("parts", [P, 2, 4, T], F32R)
        vtmp = sb("vtmp", [P, TT, D])
        v1 = sb("v1", [P, B, TT, H1, HD1 + 1])
        qstack = sb("qstack", [P, 2, PAIRS, T], F32R)
        kstack = sb("kstack", [P, 2, PAIRS, T], F32R)
        mx = sb("mx", [P, B, TT, H1])
        mxT = sb("mxT", [H1, 2, T], F32R)
        pT1 = sb("pT1", [P, H1, TT, T])
        rec1 = sb("rec1", [P, B, TT, H1])
        o1 = sb("o1", [P, TT, D])
        oT1 = sb("oT1", [P, T])

        rt = sb("rt", [1, B, NH])
        top = sb("top", [1, B, 8])
        topi = sb("topi", [1, B, 8], U32)
        negi = sb("negi", [1, B, 8])
        sorti = sb("sorti", [1, B, 8])
        heads = sb("heads", [1, B, 8], I32)
        w2h = sb("w2h", [P, 2, 3, NA * HD2])
        b2h = sb("b2h", [P, B, 2, 3])
        bq8 = sb("bq8", [P, B, 2])
        q2 = sb("q2", [P, 2, T])
        k2 = sb("k2", [P, 2, T])
        v2 = sb("v2", [P, TT, NA * HD2])
        nm2 = sb("nm2", [P, B, NA, TT])
        sum2 = sb("sum2", [P, B, TT, NA])
        rec2 = sb("rec2", [P, B, TT, NA])
        o2 = sb("o2", [P, TT, NA * HD2])
        oT2 = sb("oT2", [P, 2, T])

        lg = sb("lg", [P, B, TT, E])
        gtop = sb("gtop", [P, B, TT, 8])
        gidx = sb("gidx", [P, B, TT, 8], U32)
        gidf = sb("gidf", [P, B, TT, 2])
        nmax = sb("nmax", [P, B, TT])
        gexp = sb("gexp", [P, B, TT, E])
        gsum = sb("gsum", [P, B, TT])
        grec = sb("grec", [P, B, TT])
        m1 = sb("m1", [P, B, TT, E])
        wsel = sb("wsel", [P, B, TT, E])
        whi = sb("whi", [P, B, TT, E], F32R)
        gpack = sb("gpack", [P, B, TT, GATE_ROWS])
        gT = sb("gT", [GATE_ROWS, B, T], F32R)
        xw = sb("xw", [P, EXPERT_BUFS, T])
        hx = sb("hx", [P, EXPERT_BUFS, 2, T])
        prod = cT[:, 0:2].rearrange("p b c t -> p (b c) t")
        gs = ctok[:, 0:4, :].rearrange("p (b c) t -> p b c t", b=2)
        sg = ctok[:, 4:6, :]
        yT = ctok[:, 6:8, :]

        act_banks = [stack.enter_context(nc.psum_tensor(f"act_bank{i}", [P, 512], F32)) for i in range(RING)]
        dve_banks = [stack.enter_context(nc.psum_tensor(f"dve_bank{i}", [P, 512], F32)) for i in range(RING)]

        def abank(n):
            return act_banks[n % RING]

        def dbank(n):
            return dve_banks[n % RING]

        act_full, act_done = sem("act_full"), sem("act_done")
        dve_full, dve_done = sem("dve_full"), sem("dve_done")
        x_in = [sem(f"x_in{b}") for b in range(B)]
        cT_in = [sem(f"cT_in{b}") for b in range(B)]
        ctok_in = sem("ctok_in")
        mask_in = sem("mask_in")
        wa_in, wb_in, wc_in, we_in = sem("wa_in"), sem("wb_in"), sem("wc_in"), sem("we_in")
        lens_in, gate_rows_in, lens_cast = sem("lens_in"), sem("gate_rows_in"), sem("lens_cast")
        tanh_done = sem("tanh_done")
        gated_bias_done = sem("gated_bias_done")
        base_done = [sem(f"base_done{k}") for k in range(3)]
        rows_made = sem("rows_made")
        consts_made = sem("consts_made")
        stats_done = sem("stats_done")
        rstd_done = sem("rstd_done")
        xn_done = sem("xn_done")
        xn_read = sem("xn_read")
        parts_done = sem("parts_done")
        stack_const = [sem(f"stack_const{b}") for b in range(B)]
        stack_in = [sem(f"stack_in{b}") for b in range(B)]
        max_in = [sem(f"max_in{b}") for b in range(B)]
        v_sum_done = sem("v_sum_done")
        v1_done = sem("v1_done")
        v_ones = sem("v_ones")
        s_reduced = sem("s_reduced")
        x_done = [sem(f"x_done{k}") for k in range(4)]
        heads_done = sem("heads_done")
        head_in = [sem(f"head_in{b}") for b in range(B)]
        bq8_done = sem("bq8_done")
        exp2_done = sem("exp2_done")
        nm2_done = sem("nm2_done")
        pv1_done = sem("pv1_done")
        pv2_done = sem("pv2_done")
        pt2_read = sem("pt2_read")
        o2_read = sem("o2_read")
        gate_max_done, gate_exp_done, gpack_done = sem("gate_max_done"), sem("gate_exp_done"), sem("gpack_done")
        ssq_done, rs_done, u_done = sem("ssq_done"), sem("rs_done"), sem("u_done")
        hits_done, bound_done, pick_done = sem("hits_done"), sem("bound_done"), sem("pick_done")
        up_read = sem("up_read")
        down_read = sem("down_read")
        prod_done = sem("prod_done")
        prod_read = sem("prod_read")
        y_done = sem("y_done")
        y_read = sem("y_read")
        silu_done = sem("silu_done")
        gs_done = sem("gs_done")
        dve_chain, act_chain, pool_chain = sem("dve_chain"), sem("act_chain"), sem("pool_chain")
        out_done = [sem(f"out_done{b}") for b in range(B)]

        block = stack.enter_context(nc.Block())

        def tiles(t, b):
            return t[:, b * TT:(b + 1) * TT, :]

        def x_of(k, b):
            return tiles(resid[k], b if k == 0 else b % 2)

        @block.sync
        def _(sp):
            def load_batch(b):
                sp.dma_start(tiles(xs, b), x.rearrange("b (t p) d -> p (b t) d", p=P)[:, b * TT:(b + 1) * TT, :]
                             ).then_inc(x_in[b], 16)
                sp.dma_start(cT[:, b], ctx_feat.rearrange("(c p) (b t) -> p b c t", p=P, b=B)[:, b]
                             ).then_inc(cT_in[b], 16)

            load_batch(0)
            sp.dma_start(wa[:], pack_a).then_inc(wa_in, 16)
            sp.dma_start(wc[:], pack_c).then_inc(wc_in, 16)
            sp.dma_start(maskb[:], mask_bc.rearrange("p (b t) -> p b t", b=B)).then_inc(mask_in, 16)
            load_batch(1)

            def constant_rows(b):
                if b >= 2:
                    sp.wait_ge(act_done, ACT_AT[("st1", b - 2, H1 - 1)] + 1)
                for j in range(2):
                    r = 64 * j
                    rows = [(kstack, ROW_BIAS, bias_row[0:1, b:b + 1, :])]
                    if b < 2:
                        rows += [(qstack, ROW_BIAS, const_rows[0:1, 0:1, :]), (kstack, ROW_MAX, const_rows[0:1, 1:2, :])]
                    for dst, at, row in rows:
                        sp.dma_start(dst[r + at:r + at + 1, b % 2].bitcast(F32),
                                     row.to_broadcast([1, PAIRS, T]).bitcast(F32)).then_inc(stack_const[b], 16)

            def restack(b):
                sp.wait_ge(parts_done, 2 * (b + 1))
                for dst, sources in ((qstack, (0, 1, 0)), (kstack, (2, 2, 3))):
                    for r, s in enumerate(sources):
                        for j in range(2):
                            lo = 64 * j + HD1 * r
                            sp.dma_start(dst[lo:lo + HD1, b % 2].bitcast(F32),
                                         parts[64 * j:64 * j + 64, b % 2, s, :].bitcast(F32)).then_inc(stack_in[b], 16)

            def fetch_heads(b):
                if b >= 2:
                    sp.wait_ge(act_done, ACT_AT[("qkv2", b - 2, 0)] + 3)
                sp.wait_ge(heads_done, b + 1)
                for a in range(NA):
                    h = sp.value_load(heads[0:1, b, a:a + 1], min_val=0, max_val=NH - 1)
                    sp.dma_start(w2h[:, b % 2, :, a * HD2:(a + 1) * HD2],
                                 head_w[bass.ds(h, 1)].rearrange("h p (m d) -> (h p) m d", m=3)).then_inc(head_in[b], 16)
                    lo = HD2 * (a % 2)
                    sp.dma_start(b2h[lo:lo + HD2, b, a // 2, :],
                                 head_b[bass.ds(h, 1)].rearrange("h p m -> (h p) m")).then_inc(head_in[b], 16)

            sp.wait_ge(rows_made, 2)
            constant_rows(0)
            for step in SCHEDULE:
                what, b, i = step
                if what == "q":
                    if b > 0:
                        constant_rows(b)
                    restack(b)
                    if b == 0:
                        sp.dma_start(wb[:], pack_b).then_inc(wb_in, 16)
                        sp.dma_start(lens_i[:], lens.rearrange("p (t b) -> p t b", b=B)).then_inc(lens_in, 16)
                        sp.dma_start(ctok[:], ctx_tok.rearrange("b (t p) d -> p (b t) d", p=P)).then_inc(ctok_in, 16)
                        load_batch(2)
                        load_batch(3)
                    if b == 1:
                        sp.dma_start(we[:], pack_e).then_inc(we_in, 16)
                        sp.dma_start(sel_f, sel_in).then_inc(gate_rows_in, 16)
                        sp.dma_start(b3_f, b3_in).then_inc(gate_rows_in, 16)
                elif what == "max1":
                    sp.wait_ge(act_done, ACT_AT[step] + 1)
                    for j in range(2):
                        r = 64 * j + ROW_MAX
                        sp.dma_start(qstack[r:r + 1, b % 2].bitcast(F32),
                                     mxT[PAIRS * j:PAIRS * (j + 1), b % 2, :].bitcast(F32)).then_inc(max_in[b], 16)
                elif what == "route":
                    fetch_heads(b)
                elif what == "y4":
                    sp.wait_ge(dve_done, DVE_AT[step] + 1)
                    sp.dma_start(out.rearrange("b (t p) d -> p (b t) d", p=P)[:, b * TT:(b + 1) * TT, :],
                                 tiles(outs, b)).then_inc(out_done[b], 16)
            for b in range(B):
                sp.wait_ge(out_done[b], 16)

        @block.tensor
        def _(pe):
            def take_act(n):
                if n >= RING:
                    pe.wait_ge(act_done, n - RING + 1)
                return abank(n)

            def take_dve(n):
                if n >= RING:
                    pe.wait_ge(dve_done, n - RING + 1)
                return dbank(n)

            for step in SCHEDULE:
                what, b, i = step
                na, nd = ACT_AT[step], DVE_AT[step]
                if what == "kv":
                    if b == 0:
                        pe.wait_ge(wa_in, 16)
                    pe.wait_ge(cT_in[b], 16)
                    bank = take_dve(nd)
                    for c in range(CC):
                        mm = pe.matmul(bank[:, 0:T], A("wk")[:, c * D:(c + 1) * D], cT[:, b, c, :],
                                       start=(c == 0), stop=(c == CC - 1))
                    mm.then_inc(dve_full, 1)
                    bank = take_dve(nd + 1)
                    for t in range(TT):
                        for c in range(CC):
                            mm = pe.matmul(bank[:, t * D:(t + 1) * D], cT[:, b, c, t * P:(t + 1) * P],
                                           A("wv")[:, c * D:(c + 1) * D], start=(c == 0), stop=(c == CC - 1))
                    mm.then_inc(dve_full, 1)
                elif what == "norm":
                    if b == 0 and i == 0:
                        pe.wait_ge(wc_in, 16)
                    pe.wait_ge(xn_done, NORM_AT[step] + 1)
                    bank = take_act(na)
                    for t in range(TT):
                        mm = pe.transpose(bank[:, t * P:(t + 1) * P], xn[:, NORM_AT[step] % XN_BUFS, t, :], ident)
                    mm.then_inc(act_full, 1)
                elif what == "q":
                    pe.wait_ge(act_done, ACT_AT[("norm", b, 0)] + 1)
                    bank = take_dve(nd)
                    pe.matmul(bank[:, 0:T], A("wq"), xnT[0][:, b % 2, :], start=True, stop=True).then_inc(dve_full, 1)
                elif what == "plan_a":
                    bank = take_dve(nd)
                    pe.wait_ge(lens_cast, 1)
                    pe.matmul(bank[:, 0:B], C("tri"), lens_f[:, 0, :], start=True, stop=True)
                    pe.matmul(bank[:, B:2 * B], C("ones"), lens_f[:, 0, :], start=True, stop=False)
                    pe.matmul(bank[:, B:2 * B], C("tri"), lens_f[:, 1, :], start=False, stop=True
                              ).then_inc(dve_full, 1)
                elif what == "plan_b":
                    bank = take_dve(nd)
                    pe.wait_ge(hits_done, 1)
                    for bb in range(B):
                        for t in range(TT):
                            for c in range(TT):
                                mm = pe.matmul(bank[:, t * B + bb:t * B + bb + 1], hits[:, bb, c, t * P:(t + 1) * P],
                                               C("ones")[:, 0:1], start=(c == 0), stop=(c == TT - 1))
                    mm.then_inc(dve_full, 1)
                elif what == "plan_c":
                    pe.wait_ge(dve_done, DVE_AT[("plan_b", 0, 0)] + 1)
                    bank = take_dve(nd)
                    for t in range(TT):
                        for c in range(t + 1):
                            mm = pe.matmul(bank[:, t * P:(t + 1) * P],
                                           bound[:, c, b:b + 1].to_broadcast([P, P]),
                                           C("tri") if c == t else C("ones"), start=(c == 0), stop=(c == t))
                    mm.then_inc(dve_full, 1)
                elif what == "depool":
                    pe.wait_ge(u_done, 1)
                    bank = take_act(na)
                    pe.matmul(bank[:, 0:D], C("decay")[:, 0:P], u[:, b * TT, :], start=True, stop=True)
                    pe.matmul(bank[:, D:2 * D], C("decay")[:, P:2 * P], u[:, b * TT, :], start=True, stop=False)
                    pe.matmul(bank[:, D:2 * D], C("decay")[:, 0:P], u[:, b * TT + 1, :], start=False, stop=True
                              ).then_inc(act_full, 1)
                elif what == "s1":
                    j, pair = divmod(i, PAIRS)
                    if i == 0:
                        pe.wait_ge(stack_const[b], (6 if b < 2 else 2) * 16)
                        pe.wait_ge(stack_in[b], 12 * 16)
                    bank = take_dve(nd)
                    lo, hi = 64 * j, 64 * j + ROW_MAX
                    for t in range(TT):
                        mm = pe.matmul(bank[:, t * T:(t + 1) * T], qstack[lo:hi, b % 2, pair, t * P:(t + 1) * P],
                                       kstack[lo:hi, b % 2, pair, :], start=True, stop=True)
                    mm.then_inc(dve_full, 1)
                elif what == "max1":
                    pe.wait_ge(dve_done, DVE_AT[("s1", b, H1 - 1)] + 1)
                    bank = take_act(na)
                    for t in range(TT):
                        mm = pe.transpose(bank[0:H1, t * P:(t + 1) * P], mx[:, b, t, :], ident)
                    mm.then_inc(act_full, 1)
                elif what == "st1":
                    j, pair = divmod(i, PAIRS)
                    if i == 0:
                        pe.wait_ge(max_in[b], 2 * 16)
                    bank = take_act(na)
                    lo, hi = 64 * j, 64 * j + ROW_MAX + 1
                    for c in range(TT):
                        mm = pe.matmul(bank[:, c * T:(c + 1) * T], kstack[lo:hi, b % 2, pair, c * P:(c + 1) * P],
                                       qstack[lo:hi, b % 2, pair, :], start=True, stop=True)
                    mm.then_inc(act_full, 1)
                elif what == "pv1":
                    pe.wait_ge(v1_done, b + 1)
                    bank = take_dve(nd)
                    for h in range(H1):
                        pe.wait_ge(act_done, ACT_AT[("st1", b, h)] + 1)
                        for t in range(TT):
                            at = (t * H1 + h) * (HD1 + 1)
                            for c in range(TT):
                                mm = pe.matmul(bank[:, at:at + HD1 + 1], pT1[:, h, c, t * P:(t + 1) * P],
                                               v1[:, b, c, h, :], start=(c == 0), stop=(c == TT - 1))
                    mm.then_inc(dve_full, 1)
                elif what == "o1":
                    pe.wait_ge(dve_done, DVE_AT[("pv1", b, 0)] + 1)
                    bank = take_act(na)
                    for t in range(TT):
                        mm = pe.transpose(bank[:, t * P:(t + 1) * P], o1[:, t, :], ident)
                    mm.then_inc(act_full, 1)
                elif what == "y1":
                    if b == 0:
                        pe.wait_ge(wb_in, 16)
                    bank = take_dve(nd)
                    pe.wait_ge(act_done, ACT_AT[("o1", b, 0)] + 1)
                    for t in range(TT):
                        pe.matmul(bank[:, t * D:(t + 1) * D], xnT[0][:, b % 2, t * P:(t + 1) * P], W("wo_x"),
                                  start=True, stop=False)
                        mm = pe.matmul(bank[:, t * D:(t + 1) * D], oT1[:, t * P:(t + 1) * P], W("wo_u"),
                                       start=False, stop=True)
                    mm.then_inc(dve_full, 1)
                elif what == "route":
                    pe.wait_ge(act_done, ACT_AT[("norm", b, 1)] + 1)
                    bank = take_dve(nd)
                    pe.matmul(bank[0:1, 0:NH], xsum[:, b:b + 1], W("wr"), start=True, stop=True
                              ).then_inc(dve_full, 1)
                elif what == "qkv2":
                    pe.wait_ge(head_in[b], 8 * 16)
                    for m in range(2):
                        bank = take_act(na + m)
                        for g in range(2):
                            mm = pe.matmul(bank[:, g * T:(g + 1) * T],
                                           w2h[:, b % 2, m, g * P:(g + 1) * P], xnT[1][:, b % 2, :],
                                           start=True, stop=True)
                        mm.then_inc(act_full, 1)
                    bank = take_act(na + 2)
                    for t in range(TT):
                        mm = pe.matmul(bank[:, t * NA * HD2:(t + 1) * NA * HD2], xnT[1][:, b % 2, t * P:(t + 1) * P],
                                       w2h[:, b % 2, 2, :], start=True, stop=True)
                    mm.then_inc(act_full, 1)
                elif what == "s2":
                    if i == 0:
                        pe.wait_ge(act_done, ACT_AT[("qkv2", b, 0)] + 2)
                    bank = take_act(na)
                    lo, g = HD2 * (i % 2), i // 2
                    for t in range(TT):
                        mm = pe.matmul(bank[:, t * T:(t + 1) * T], q2[lo:lo + HD2, g, t * P:(t + 1) * P],
                                       k2[lo:lo + HD2, g, :], start=True, stop=True)
                    mm.then_inc(act_full, 1)
                elif what == "pt2":
                    pe.wait_ge(act_done, ACT_AT[("s2", b, i)] + 1)
                    bank = take_dve(nd)
                    for c in range(TT):
                        for t in range(TT):
                            mm = pe.transpose(bank[:, c * T + t * P:c * T + (t + 1) * P],
                                              p2[:, i, t, c * P:(c + 1) * P], ident)
                    mm.then_inc(dve_full, 1)
                elif what == "pv2":
                    pe.wait_ge(act_done, ACT_AT[("qkv2", b, 0)] + 3)
                    bank = take_dve(nd)
                    for a in range(NA):
                        pe.wait_ge(dve_done, DVE_AT[("pt2", b, a)] + 1)
                        for t in range(TT):
                            at = (t * NA + a) * HD2
                            for c in range(TT):
                                mm = pe.matmul(bank[:, at:at + HD2], pT2[:, a, c, t * P:(t + 1) * P],
                                               v2[:, c, a * HD2:(a + 1) * HD2], start=(c == 0), stop=(c == TT - 1))
                    mm.then_inc(dve_full, 1)
                elif what == "o2":
                    pe.wait_ge(dve_done, DVE_AT[("pv2", b, 0)] + 1)
                    bank = take_act(na)
                    for g in range(2):
                        for t in range(TT):
                            mm = pe.transpose(bank[:, g * T + t * P:g * T + (t + 1) * P],
                                              o2[:, t, g * P:(g + 1) * P], ident)
                    mm.then_inc(act_full, 1)
                elif what == "y2":
                    pe.wait_ge(act_done, ACT_AT[("o2", b, 0)] + 1)
                    bank = take_dve(nd)
                    for t in range(TT):
                        for g in range(2):
                            mm = pe.matmul(bank[:, t * D:(t + 1) * D], oT2[:, g, t * P:(t + 1) * P],
                                           W("wo2")[:, g * D:(g + 1) * D], start=(g == 0), stop=(g == 1))
                    mm.then_inc(dve_full, 1)
                elif what == "y3":
                    if b == 0:
                        pe.wait_ge(consts_made, 1)
                    pe.wait_ge(act_done, max(ACT_AT[("norm", b, 2)], ACT_AT[("depool", b, 0)]) + 1)
                    pe.wait_ge(dve_done, DVE_AT[("plan_c", b, 0)] + 1)
                    bank = take_dve(nd)
                    for t in range(TT):
                        pe.matmul(bank[:, t * D:(t + 1) * D], xnT[2][:, b % 2, t * P:(t + 1) * P], w_in_g[:],
                                  start=True, stop=False)
                        for c in range(TT):
                            mm = pe.matmul(bank[:, t * D:(t + 1) * D], pick[:, b % 2, c, t * P:(t + 1) * P],
                                           dp[:, b, c, :], start=False, stop=(c == TT - 1))
                    mm.then_inc(dve_full, 1)
                elif what == "gate":
                    if b == 0:
                        pe.wait_ge(we_in, 16)
                    pe.wait_ge(act_done, ACT_AT[("norm", b, 3)] + 1)
                    bank = take_dve(nd)
                    for t in range(TT):
                        mm = pe.matmul(bank[:, t * E:(t + 1) * E], xnT[3][:, b % 2, t * P:(t + 1) * P], X("gate"),
                                       start=True, stop=True)
                    mm.then_inc(dve_full, 1)
                elif what == "gate_t":
                    pe.wait_ge(gpack_done, b + 1)
                    bank = take_act(na)
                    for t in range(TT):
                        mm = pe.transpose(bank[0:GATE_ROWS, t * P:(t + 1) * P], gpack[:, b, t, :], ident)
                    mm.then_inc(act_full, 1)
                elif what == "wide":
                    if i == 0:
                        if b == 0:
                            pe.wait_ge(consts_made, 3)
                        pe.wait_ge(act_done, ACT_AT[("gate_t", b, 0)] + 1)
                    bank = take_dve(nd)
                    pe.matmul(bank[:, 0:T], sel[:, i, :], gT[:, b, :], start=True, stop=True).then_inc(dve_full, 1)
                elif what == "up":
                    bank = take_act(na)
                    pe.wait_ge(dve_done, DVE_AT[("wide", b, i)] + 1)
                    xe = xw[:, (b * E + i) % EXPERT_BUFS, :]
                    pe.matmul(bank[:, 0:T], X("w1")[:, i * D:(i + 1) * D], xe, start=True, stop=True)
                    pe.matmul(bank[:, T:2 * T], X("w3")[:, i * D:(i + 1) * D], xe, start=True, stop=False
                              ).then_inc(up_read, 1)
                    pe.matmul(bank[:, T:2 * T], b3s[:, i, :], gT[:, b, :], start=False, stop=True
                              ).then_inc(act_full, 1)
                elif what == "down":
                    pe.wait_ge(act_done, ACT_AT[("up", b, i)] + 1)
                    bank = take_dve(nd)
                    pe.matmul(bank[:, 0:T], X("w2")[:, i * D:(i + 1) * D], hx[:, (b * E + i) % EXPERT_BUFS, 0, :],
                              start=True, stop=True).then_inc(dve_full, 1)
                elif what == "shared":
                    for m, (name, bank) in enumerate((("sw1", take_act(na)), ("sw2", take_dve(nd)))):
                        for c in range(HALVES):
                            mm = pe.matmul(bank[:, c * T:(c + 1) * T], X(name)[:, c * P:(c + 1) * P], xnT[3][:, b % 2, :],
                                           start=True, stop=True)
                        mm.then_inc((act_full, dve_full)[m], 1)
                elif what == "y4":
                    bank = take_dve(nd)
                    pe.wait_ge(dve_done, DVE_AT[("shared", b, 0)] + 1)
                    pe.wait_ge(prod_read, E * (b + 1))
                    for t in range(TT):
                        for c in range(HALVES):
                            pe.matmul(bank[:, t * D:(t + 1) * D], gs[:, b % 2, c, t * P:(t + 1) * P],
                                      X("sw3")[:, c * D:(c + 1) * D], start=(c == 0), stop=False)
                        mm = pe.matmul(bank[:, t * D:(t + 1) * D], yT[:, b % 2, t * P:(t + 1) * P], ident,
                                       start=False, stop=True)
                    mm.then_inc(dve_full, 1)

        @block.scalar
        def _(act):
            for step in SCHEDULE:
                what, b, i = step
                n = ACT_AT[step]
                bank = abank(n)
                if USES[what][0] and what not in ("qkv2",):
                    act.wait_ge(act_full, n + 1)
                if what == "plan_a":
                    act.wait_ge(wb_in, 16)
                    act.activation(tg[:], W("gates"), ACT.Tanh).then_inc(tanh_done, 1)
                    act.wait_ge(ctok_in, 16)
                    for m in range(B * TT):
                        if m >= 2:
                            act.wait_ge(ssq_done, m - 1)
                        act.activation(sq_junk[:, m % 2, :], ctok[:, m, :], ACT.Square, accum_out=ssq[:, m:m + 1]
                                       ).then_inc(ssq_done, 1)
                elif what == "norm":
                    if i == 1:
                        act.activation(xnT[1][:, b % 2, :], bank[:, 0:T], ACT.Identity, accum_out=xsum[:, b:b + 1]
                                       ).then_inc(act_done, 1)
                    else:
                        act.copy(xnT[i][:, b % 2, :], bank[:, 0:T]).then_inc(act_done, 1)
                elif what == "depool":
                    act.copy(dp[:, b].rearrange("p c d -> p (c d)"), bank[:, 0:TT * D]).then_inc(act_done, 1)
                elif what == "max1":
                    act.copy(mxT[:, b % 2, :], bank[0:H1, 0:T]).then_inc(act_done, 1)
                elif what == "st1":
                    if i == 0 and b >= 1:
                        act.wait_ge(dve_done, DVE_AT[("pv1", b - 1, 0)] + 1)
                    act.activation(pT1[:, i].rearrange("p c t -> p (c t)"), bank[:], ACT.Exp, scale=HD1 ** -0.5).then_inc(act_done, 1)
                elif what == "o1":
                    act.copy(oT1[:], bank[:, 0:T]).then_inc(act_done, 1)
                elif what == "qkv2":
                    act.wait_ge(head_in[b], 8 * 16)
                    act.wait_ge(bq8_done, b + 1)
                    act.wait_ge(act_full, n + 1)
                    for g in range(2):
                        ins = act.activation(q2[:, g, :], abank(n)[:, g * T:(g + 1) * T], ACT.Identity,
                                             scale=HD2 ** -0.5, bias=bq8[:, b, g:g + 1])
                    ins.then_inc(act_done, 1)
                    act.wait_ge(act_full, n + 2)
                    for g in range(2):
                        ins = act.activation(k2[:, g, :], abank(n + 1)[:, g * T:(g + 1) * T], ACT.Identity,
                                             bias=b2h[:, b, g, 1:2])
                    ins.then_inc(act_done, 1)
                    act.wait_ge(act_full, n + 3)
                    act.copy(v2[:].rearrange("p t d -> p (t d)"), abank(n + 2)[:]).then_inc(act_done, 1)
                elif what == "s2":
                    act.wait_ge(nm2_done, NA * b + i + 1)
                    if b >= 1:
                        act.wait_ge(dve_done, DVE_AT[("pt2", b - 1, i)] + 1)
                    for t in range(TT):
                        ins = act.activation(p2[:, i, t, :], bank[:, t * T:(t + 1) * T], ACT.Exp,
                                             bias=nm2[:, b, i, t:t + 1], accum_out=sum2[:, b, t, i:i + 1])
                    ins.then_inc(act_done, 1)
                elif what == "o2":
                    for g in range(2):
                        ins = act.activation(oT2[:, g, :], bank[:, g * T:(g + 1) * T], ACT.Identity,
                                             bias=b2h[:, b, g, 2:3])
                    ins.then_inc(act_done, 1)
                elif what == "gate":
                    act.wait_ge(gate_max_done, b + 1)
                    for t in range(TT):
                        ins = act.activation(gexp[:, b, t, :], lg[:, b, t, :], ACT.Exp, bias=nmax[:, b, t:t + 1],
                                             accum_out=gsum[:, b, t:t + 1])
                    ins.then_inc(gate_exp_done, 1)
                elif what == "gate_t":
                    act.copy(gT[:, b, :], bank[0:GATE_ROWS, 0:T]).then_inc(act_done, 1)
                elif what == "up":
                    k = b * E + i
                    if k >= EXPERT_BUFS:
                        act.wait_ge(dve_done, DVE_AT[expert(k - EXPERT_BUFS)] + 1)
                    act.activation(hx[:, k % EXPERT_BUFS, 0, :], bank[:, 0:T], ACT.Silu, bias=X("b1")[:, i:i + 1])
                    act.copy(hx[:, k % EXPERT_BUFS, 1, :], bank[:, T:2 * T]).then_inc(act_done, 1)
                elif what == "shared":
                    if b >= 1:
                        act.wait_ge(dve_done, DVE_AT[("shared", b - 1, 0)] + 1)
                    act.activation(sg.rearrange("p c t -> p (c t)"), bank[:], ACT.Silu).then_inc(act_done, 1)

        @block.vector
        def _(dve):
            chained = [0]

            def link(ins):
                chained[0] += 1
                ins.then_inc(dve_chain, 1)
                dve.wait_ge(dve_chain, chained[0])

            link(dve.memset(negi[:], -100.0))
            dve.memset(v1[:], 1.0).then_inc(v_ones, 1)
            link(dve.memset(qkf[:, 0, :], 1.0))
            link(dve.tensor_copy(const_rows[0:1, 0, :], qkf[0:1, 0, :]))
            dve.tensor_scalar(const_rows[0:1, 1, :], qkf[0:1, 0, :], -1.0, None, ALU.mult).then_inc(rows_made, 1)
            dve.wait_ge(rows_made, 1)
            dve.wait_ge(mask_in, 16)
            dve.tensor_scalar(bias_row[:], maskb[0:1], 0.0, MASKED,
                              ALU.is_equal, ALU.mult).then_inc(rows_made, 1)

            def make_consts():
                dve.wait_ge(wb_in, 16)
                dve.tensor_scalar(w_in_g[:], W("w_in"), W("g_res"), None, ALU.mult).then_inc(consts_made, 1)

            def make_gate_rows():
                dve.wait_ge(gate_rows_in, 32)
                dve.tensor_copy(sel[:].rearrange("p e n -> p (e n)"), sel_f).then_inc(consts_made, 1)
                link(dve.tensor_copy(b3_hi, b3_f))
                dve.scalar_tensor_tensor(out=b3s[:].rearrange("p e n -> p (e n)"), in0=b3_hi.bitcast(F32),
                                         scalar=C("alpha")[0:GATE_ROWS, :], in1=b3_f, op0=ALU.mult, op1=ALU.add
                                         ).then_inc(consts_made, 1)

            def split(step, k):
                b = step[1]
                if b >= 2:
                    dve.wait_ge(stack_in[b - 2], 12 * 16)
                link(dve.tensor_copy(parts[:, b % 2, 2 * k, :], qkf[:, k, :]))
                dve.tensor_tensor(parts[:, b % 2, 2 * k + 1, :], qkf[:, k, :], parts[:, b % 2, 2 * k, :].bitcast(F32),
                                  ALU.subtract).then_inc(parts_done, 1)
                dve.wait_ge(parts_done, PARTS_AT[step] + 1)

            def project(step, k, name, n):
                dve.wait_ge(dve_full, n + 1)
                dve.scalar_tensor_tensor(out=qkf[:, k, :], in0=dbank(n)[:, 0:T], scalar=A(name),
                                         in1=maskb[:, step[1], :], op0=ALU.add, op1=ALU.mult).then_inc(dve_done, 1)
                dve.wait_ge(dve_done, n + 1)
                split(step, k)

            def residual(k, b, bank, done):
                if k < 3:
                    dve.wait_ge(base_done[k], b + 1)
                before = base[k][:, b % 2] if k < 3 else x_of(3, b)
                if k < 2 and b >= 2:
                    dve.wait_ge(base_done[k + 1], b - 1)
                after = x_of(k + 1, b) if k < 3 else tiles(outs, b)
                dve.scalar_tensor_tensor(out=after, in0=bank[:, 0:TT * D].rearrange("p (t d) -> p t d", t=TT),
                                         scalar=tg[:, k:k + 1], in1=before, op0=ALU.mult, op1=ALU.add
                                         ).then_inc(dve_done, 1)

            for step in SCHEDULE:
                what, b, i = step
                n = DVE_AT[step]
                bank = dbank(n)
                if USES[what][1] and what not in ("kv", "q", "plan_a"):
                    dve.wait_ge(dve_full, n + 1)
                if what == "stat":
                    if i == 0:
                        dve.wait_ge(x_in[b], 16)
                    else:
                        dve.wait_ge(dve_done, DVE_AT[(f"y{i}", b, 0)] + 1)
                    for t in range(TT):
                        ins = dve.bn_stats(st[:, b, i, t, :], x_of(i, b)[:, t, :])
                    link(ins)
                    for t in range(TT):
                        ins = dve.bn_aggr(mv[:, b, i, t, :], st[:, b, i, t, :])
                    ins.then_inc(stats_done, 1)
                elif what == "norm":
                    k = NORM_AT[step]
                    dve.wait_ge(rstd_done, STAT_AT[("stat", b, i)] + 1)
                    if k >= XN_BUFS:
                        dve.wait_ge(act_done, ACT_AT[NORMS[k - XN_BUFS]] + 1)
                    for t in range(TT):
                        ins = dve.tensor_scalar(xn[:, k % XN_BUFS, t, :], x_of(i, b)[:, t, :],
                                                mv[:, b, i, t, 0:1], rstd[:, b, i, t:t + 1],
                                                ALU.subtract, ALU.mult)
                    ins.then_inc(xn_done, 1)
                elif what == "kv":
                    if b == 0:
                        dve.wait_ge(wa_in, 16)
                    project(step, 1, "bk", n)
                    dve.wait_ge(dve_full, n + 2)
                    if b >= 1:
                        dve.wait_ge(v1_done, b)
                    dve.tensor_tensor(vtmp[:], dbank(n + 1)[:, 0:TT * D].rearrange("p (t d) -> p t d", t=TT),
                                      A("bv").unsqueeze(1).to_broadcast([P, TT, D]), ALU.add).then_inc(dve_done, 1)
                elif what == "q":
                    project(step, 0, "bq", n)
                elif what == "plan_a":
                    dve.wait_ge(lens_in, 16)
                    dve.tensor_copy(lens_f[:], lens_i[:]).then_inc(lens_cast, 1)
                    dve.wait_ge(dve_full, n + 1)
                    dve.tensor_scalar(bidx[:].rearrange("p t b -> p (t b)"), bank[:, 0:TT * B], -1.0, None,
                                      ALU.add).then_inc(dve_done, 1)
                    dve.wait_ge(dve_done, n + 1)
                    link(dve.tensor_scalar(wrapped[:], bidx[:], 0.0, float(T), ALU.is_lt, ALU.mult))
                    link(dve.tensor_tensor(wrapped[:], bidx[:], wrapped[:], ALU.add))
                    for bb in range(B):
                        for c in range(TT):
                            ins = dve.tensor_scalar(hits[:, bb, c, :], C("position"), wrapped[:, c, bb:bb + 1], None,
                                                    ALU.is_equal)
                    ins.then_inc(hits_done, 1)
                    make_consts()
                elif what == "plan_b":
                    dve.tensor_scalar(bound[:].rearrange("p t b -> p (t b)"), bank[:, 0:TT * B], 1.0, None,
                                      ALU.min).then_inc(dve_done, 1)
                elif what == "plan_c":
                    for c in range(TT):
                        ins = dve.tensor_scalar(pick[:, b % 2, c, :], bank[:, 0:T], 1.0, C("row")[:, c:c + 1],
                                                ALU.max, ALU.is_equal)
                    ins.then_inc(dve_done, 1)
                elif what == "u":
                    dve.wait_ge(rs_done, 1)
                    for m in range(B * TT):
                        ins = dve.scalar_tensor_tensor(out=u[:, m, :], in0=ctok[:, m, 0:D], scalar=rs[:, m:m + 1],
                                                       in1=W("g_init"), op0=ALU.mult, op1=ALU.mult)
                    ins.then_inc(u_done, 1)
                    make_gate_rows()
                elif what == "s1":
                    dve.tensor_reduce(mx[:, b, :, i], bank[:].rearrange("p (t s) -> p t s", t=TT), AX.X, ALU.max
                                      ).then_inc(dve_done, 1)
                elif what == "pv1":
                    heads_out = bank[:, 0:TT * H1 * (HD1 + 1)].rearrange("p (t h d) -> p t h d", t=TT, h=H1)
                    link(dve.reciprocal(rec1[:, b], heads_out[:, :, :, HD1]))
                    dve.tensor_tensor(o1[:].rearrange("p t (h d) -> p t h d", h=H1), heads_out[:, :, :, 0:HD1],
                                      rec1[:, b].unsqueeze(3).to_broadcast([P, TT, H1, HD1]), ALU.mult
                                      ).then_inc(dve_done, 1)
                elif what in ("y1", "y2", "y3", "y4"):
                    if what == "y1" and b == 0:
                        dve.wait_ge(tanh_done, 1)
                    residual(int(what[1]) - 1, b, bank, n + 1)
                elif what == "route":
                    dve.scalar_tensor_tensor(out=rt[:, b, :], in0=bank[0:1, 0:NH], scalar=1.0 / T,
                                             in1=W("br")[0:1, :], op0=ALU.mult, op1=ALU.add).then_inc(dve_done, 1)
                    dve.wait_ge(dve_done, n + 1)
                    link(dve.max(top[:, b, :], rt[:, b, :]))
                    link(dve.max_index(topi[:, b, :], top[:, b, :], rt[:, b, :]))
                    link(dve.tensor_scalar(negi[:, b, 0:NA], topi[:, b, 0:NA], -1.0, None, ALU.mult))
                    link(dve.max(sorti[:, b, :], negi[:, b, :]))
                    dve.tensor_scalar(heads[:, b, :], sorti[:, b, :], -1.0, None, ALU.mult).then_inc(heads_done, 1)
                elif what == "s2":
                    m = ACT_AT[step]
                    dve.wait_ge(act_full, m + 1)
                    dve.tensor_reduce(nm2[:, b, i, :], abank(m)[:].rearrange("p (t s) -> p t s", t=TT), AX.X, ALU.max,
                                      negate=True).then_inc(nm2_done, 1)
                elif what == "pt2":
                    dve.tensor_copy(pT2[:, i].rearrange("p c t -> p (c t)"), bank[:]).then_inc(dve_done, 1)
                elif what == "pv2":
                    dve.wait_ge(act_done, ACT_AT[("s2", b, NA - 1)] + 1)
                    link(dve.reciprocal(rec2[:, b], sum2[:, b]))
                    dve.tensor_tensor(o2[:].rearrange("p t (a d) -> p (t a) d", a=NA),
                                      bank[:].rearrange("p (n d) -> p n d", d=HD2),
                                      rec2[:, b].rearrange("p t a -> p (t a)").unsqueeze(2).to_broadcast(
                                          [P, TT * NA, HD2]), ALU.mult).then_inc(dve_done, 1)
                elif what == "gate":
                    dve.tensor_copy(lg[:, b].rearrange("p t e -> p (t e)"), bank[:, 0:TT * E]).then_inc(dve_done, 1)
                    dve.wait_ge(dve_done, n + 1)
                    for t in range(TT):
                        ins = dve.max(gtop[:, b, t, :], lg[:, b, t, :])
                    link(ins)
                    dve.tensor_scalar(nmax[:, b, :], gtop[:, b, :, 0], -1.0, None, ALU.mult
                                      ).then_inc(gate_max_done, 1)
                    for t in range(TT):
                        ins = dve.max_index(gidx[:, b, t, :], gtop[:, b, t, :], lg[:, b, t, :])
                    link(ins)
                    link(dve.tensor_copy(gidf[:, b], gidx[:, b, :, 0:2]))
                    iota = C("position")[:, 0:E]
                    for t in range(TT):
                        ins = dve.tensor_scalar(m1[:, b, t, :], iota, gidf[:, b, t, 0:1], None, ALU.is_equal)
                    link(ins)
                    for t in range(TT):
                        ins = dve.scalar_tensor_tensor(out=gpack[:, b, t, 2 * E:3 * E], in0=iota,
                                                       scalar=gidf[:, b, t, 1:2], in1=m1[:, b, t, :],
                                                       op0=ALU.is_equal, op1=ALU.add)
                    link(ins)
                    dve.wait_ge(gate_exp_done, b + 1)
                    link(dve.reciprocal(grec[:, b], gsum[:, b]))
                    for t in range(TT):
                        ins = dve.scalar_tensor_tensor(out=wsel[:, b, t, :], in0=gexp[:, b, t, :],
                                                       scalar=grec[:, b, t:t + 1], in1=gpack[:, b, t, 2 * E:3 * E],
                                                       op0=ALU.mult, op1=ALU.mult)
                    link(ins)
                    link(dve.tensor_copy(whi[:, b], wsel[:, b]))
                    dve.tensor_copy(gpack[:, b, :, 3 * E:4 * E], gpack[:, b, :, 2 * E:3 * E])
                    dve.tensor_copy(gpack[:, b, :, 0:E], whi[:, b].bitcast(F32))
                    dve.tensor_tensor(gpack[:, b, :, E:2 * E], wsel[:, b], whi[:, b].bitcast(F32), ALU.subtract
                                      ).then_inc(gpack_done, 1)
                elif what == "wide":
                    k = b * E + i
                    if k >= EXPERT_BUFS:
                        dve.wait_ge(up_read, k - EXPERT_BUFS + 1)
                    dve.wait_ge(act_done, ACT_AT[("norm", b, 3)] + 1)
                    dve.tensor_tensor(xw[:, k % EXPERT_BUFS, :], xnT[3][:, b % 2, :], bank[:, 0:T], ALU.mult
                                      ).then_inc(dve_done, 1)
                elif what == "down":
                    k = b * E + i
                    dve.wait_ge(act_done, ACT_AT[("up", b, i)] + 1)
                    if k >= EXPERT_BUFS:
                        dve.wait_ge(prod_read, k - EXPERT_BUFS + 1)
                    dve.scalar_tensor_tensor(out=prod[:, k % EXPERT_BUFS, :], in0=bank[:, 0:T],
                                             scalar=X("b2")[:, i:i + 1], in1=hx[:, k % EXPERT_BUFS, 1, :],
                                             op0=ALU.add, op1=ALU.mult).then_inc(dve_done, 1)
                elif what == "shared":
                    dve.wait_ge(act_done, ACT_AT[step] + 1)
                    dve.tensor_tensor(gs[:, b % 2].rearrange("p c t -> p (c t)"), bank[:],
                                      sg.rearrange("p c t -> p (c t)"), ALU.mult).then_inc(dve_done, 1)

        @block.gpsimd
        def _(pool):
            chained = [0]

            def link(ins):
                chained[0] += 1
                ins.then_inc(pool_chain, 1)
                pool.wait_ge(pool_chain, chained[0])

            link(pool.memset(half[:], -0.5))
            link(pool.memset(half8[:], -0.5))
            for step in SCHEDULE:
                what, b, i = step
                if what == "stat":
                    pool.wait_ge(stats_done, STAT_AT[step] + 1)
                    mul, add = (1.0 + EPS, EPS * EPS) if i == 2 else (1.0, EPS)
                    link(pool.tensor_scalar(veps[:, b, i, :], mv[:, b, i, :, 1], mul, add, ALU.mult, ALU.add))
                    pool.tensor_tensor(rstd[:, b, i, :], veps[:, b, i, :], half[:], ALU.pow).then_inc(rstd_done, 1)
                    if i in (1, 2):
                        pool.wait_ge(dve_done, DVE_AT[(f"y{i}", b, 0)] + 1)
                        if b >= 2:
                            pool.wait_ge(dve_done, DVE_AT[(f"y{i + 1}", b - 2, 0)] + 1)
                        pool.tensor_tensor(base[i][:, b % 2], x_of(i, b),
                                           gated_bias[:, i:i + 1, :].to_broadcast([P, TT, D]), ALU.add
                                           ).then_inc(base_done[i], 1)
                elif what == "kv":
                    pool.wait_ge(wa_in, 16)
                    pool.wait_ge(v_ones, 1)
                    pool.wait_ge(dve_done, DVE_AT[step] + 2)
                    for t in range(TT):
                        ins = pool.tensor_scalar(v1[:, b, t, :, 0:HD1], vtmp[:, t, :].rearrange("p (h d) -> p h d", h=H1),
                                                 A("mask_col")[:, b * TT + t:b * TT + t + 1], None, ALU.mult)
                    ins.then_inc(v1_done, 1)
                elif what == "plan_a":
                    pool.wait_ge(wb_in, 16)
                    pool.wait_ge(tanh_done, 1)
                    for k, name in enumerate(("b_out", "bo", "b_in")):
                        ins = pool.tensor_scalar(gated_bias[:, k, :], W(name), tg[:, k:k + 1], None, ALU.mult)
                    link(ins)
                    pool.wait_ge(ssq_done, B * TT)
                    link(pool.tensor_scalar(ms[:], ssq[:], 1.0 / DC, EPS, ALU.mult, ALU.add))
                    pool.tensor_tensor(rs[:], ms[:], half8[:], ALU.pow).then_inc(rs_done, 1)
                elif what == "s1" and i == 0:
                    pool.wait_ge(x_in[b], 16)
                    if b >= 2:
                        pool.wait_ge(dve_done, DVE_AT[("y1", b - 2, 0)] + 1)
                    pool.tensor_tensor(base[0][:, b % 2], tiles(xs, b), gated_bias[:, 0:1, :].to_broadcast([P, TT, D]),
                                       ALU.add).then_inc(base_done[0], 1)
                elif what == "qkv2":
                    pool.wait_ge(head_in[b], 8 * 16)
                    pool.tensor_scalar(bq8[:, b, :], b2h[:, b, :, 0], HD2 ** -0.5, None, ALU.mult
                                       ).then_inc(bq8_done, 1)
                elif what == "down":
                    k = b * E + i
                    pool.wait_ge(dve_done, DVE_AT[step] + 1)
                    if i == 0:
                        if b >= 2:
                            pool.wait_ge(dve_done, DVE_AT[("y4", b - 2, 0)] + 1)
                        ins = pool.tensor_copy(yT[:, b % 2, :], prod[:, k % EXPERT_BUFS, :])
                    else:
                        pool.wait_ge(prod_read, k)
                        ins = pool.tensor_tensor(yT[:, b % 2, :], yT[:, b % 2, :], prod[:, k % EXPERT_BUFS, :],
                                                 ALU.add)
                    ins.then_inc(prod_read, 1)


def kernel(**inputs):
    import math

    import numpy as np
    import concourse.bacc as bacc
    from concourse.bass_utils import run_bass_kernel_spmd

    g = {k: np.asarray(v) for k, v in inputs.items()}
    f = np.float32

    def rows(v):
        return np.broadcast_to(v.reshape(1, -1), (P, v.size))

    def stacked(w, n):
        return w.reshape(n, P, -1).transpose(1, 0, 2).reshape(P, -1)

    def pack(fields, width, **parts):
        packed = np.zeros((P, width), f)
        for name, (lo, hi) in fields.items():
            packed[:, lo:hi] = parts[name]
        return packed

    order = np.arange(D).reshape(2, PAIRS, HD1).transpose(0, 2, 1).reshape(-1)
    w_src, w_out = g["L0_xattn_W_src"], g["L0_xattn_W_out"]
    mask = g["mask_BxS2_fk1"]
    pack_a = pack(PACK_A, PACK_A_W,
                  wk=stacked(w_src[:D][order].T, CC), wv=stacked(w_src[D:].T, CC),
                  wq=g["L0_xattn_W_tgt"][order].T, bq=g["L0_xattn_b_tgt"][order][:, None],
                  bk=g["L0_xattn_b_src"][:D][order][:, None], bv=rows(g["L0_xattn_b_src"][D:]),
                  mask_col=mask.reshape(B * TT, P).T)
    pack_b = pack(PACK_B, PACK_B_W,
                  wo_x=w_out[:, :D].T, wo_u=w_out[:, D:].T, b_out=rows(g["L0_xattn_b_out"]),
                  wr=g["L0_ffn_Wr"], br=rows(g["L0_ffn_br"]), wo2=stacked(g["L0_ffn_Wo"], 2), bo=rows(g["L0_ffn_bo"]),
                  w_in=g["L1_xattn_W_in"].T, b_in=rows(g["L1_xattn_b_in"]), g_res=g["L1_xattn_g_res"][:, None],
                  g_init=rows(g["L1_xattn_g_init"][:D]),
                  gates=rows(np.array([g["g_xattn"][0], g["g_ffn"][0], g["g_xattn"][1], g["g_ffn"][1]], f)))

    a = -math.expm1(-0.001)
    k = np.arange(P)
    near = k[None, :] - k[:, None]
    decay_near = np.where(near >= 0, math.exp(-0.001) * a ** np.maximum(near, 0).astype(float), 0.0)
    decay_far = math.exp(-0.001) * a ** (P + near).astype(float)
    pack_c = pack(PACK_C, PACK_C_W,
                  ident=np.eye(P), tri=(near >= 0), ones=1.0,
                  decay=np.concatenate([decay_near, decay_far, np.zeros((P, P))], 1),
                  position=rows(np.arange(T)), row=np.stack([k + 1, k + 1 + P], 1),
                  alpha=np.where(k >= 3 * E, -1.0, 0.0)[:, None])

    def experts(w):
        return w.transpose(2, 0, 1).reshape(P, -1)

    pack_e = pack(PACK_E, PACK_E_W,
                  gate=g["L1_ffn_gate_w"].T, b1=g["L1_ffn_b1"].T, b2=g["L1_ffn_b2"].T,
                  sw1=g["L1_ffn_sw1"].T, sw2=g["L1_ffn_sw2"].T, sw3=stacked(g["L1_ffn_sw3"].T, HALVES),
                  w1=experts(g["L1_ffn_w1"]), w3=experts(g["L1_ffn_w3"]), w2=experts(g["L1_ffn_w2"]))
    sel = np.zeros((GATE_ROWS, E, P), f)
    b3 = np.zeros((GATE_ROWS, E, P), f)
    for e in range(E):
        sel[e, e] = sel[E + e, e] = 1.0
        b3[2 * E + e, e] = b3[3 * E + e, e] = g["L1_ffn_b3"][e]

    heads = [g[f"L0_ffn_W{n}"].reshape(D, NH, HD2).transpose(1, 0, 2) for n in "qkv"]
    head_biases = [g[f"L0_ffn_b{n}"].reshape(NH, HD2, 1) for n in "qkv"]
    arrays = {
        "x_tokens": g["x"], "ctx_tokens": g["ctx_2048"],
        "ctx_features": np.ascontiguousarray(g["ctx_2048"].reshape(B * T, DC).T),
        "pack_a": pack_a, "pack_b": pack_b, "pack_c": pack_c, "pack_e": pack_e,
        "mask_everywhere": np.ascontiguousarray(rows(mask)), "mask_rows": mask.reshape(1, -1),
        "patch_lens": np.ascontiguousarray(g["mask_BxS2_if0"].reshape(B, TT, P).transpose(2, 1, 0).reshape(P, -1)),
        "head_weights": np.ascontiguousarray(np.concatenate(heads, 2)),
        "head_bias": np.ascontiguousarray(np.concatenate(head_biases, 2)),
        "gate_selectors": sel.reshape(GATE_ROWS, -1), "gate_biases": b3.reshape(GATE_ROWS, -1),
    }
    nc = bacc.Bacc("TRN2", target_bir_lowering=False, num_devices=1)
    args = [nc.dram_tensor(name, v.shape, mybir.dt.from_np(v.dtype), kind="ExternalInput").ap()
            for name, v in arrays.items()]
    out = nc.dram_tensor("out_tokens", (B, T, D), F32, kind="ExternalOutput").ap()
    flamingo(nc, *args, out)
    result = run_bass_kernel_spmd(nc, [arrays], core_ids=[0])
    return result.results[0]["out_tokens"]
```

```python
from contextlib import ExitStack

import concourse.bass as bass
from concourse import mybir

F32 = mybir.dt.float32
F32R = mybir.dt.float32r
BF16 = mybir.dt.bfloat16
I32 = mybir.dt.int32
U32 = mybir.dt.uint32
ALU = mybir.AluOpType
ACT = mybir.ActivationFunctionType
AX = mybir.AxisListType

P = 128
B = 4
T = 256
TT = T // P
D = 128
DC = 256
CC = DC // P
H1, HD1 = 8, 16
PAIRS = H1 // 2
NH, NA, HD2 = 16, 4, 64
E = 8
HALVES = 2
EPS = 1e-5
MASKED = -1e30
ACT_RING, DVE_RING = 3, 5

STACK = 3 * HD1
ROW_BIAS = STACK
ROW_MAX = STACK + 1

USES = {
    "gates": (0, 0), "plan_a": (0, 1), "plan_b": (0, 1), "plan_c": (0, 1), "u": (0, 0), "consts": (0, 0),
    "depool": (1, 0),
    "kv": (0, 2), "q": (0, 1),
    "stat": (0, 0), "norm": (1, 0),
    "s1": (0, 1), "max1": (1, 0), "st1": (1, 0), "pv1": (1, 0), "heads1": (0, 1), "o1": (1, 0), "y1": (0, 1),
    "route": (0, 1), "qkv2": (3, 0), "s2": (1, 0), "scale2": (0, 0), "pt2": (0, 1), "pv2": (1, 0), "y2": (0, 1),
    "y3": (0, 1),
    "gate": (0, 1), "gate_t": (1, 0), "wide": (0, 1), "up": (1, 0), "down": (0, 1),
    "shared": (1, 1), "y4": (0, 1),
}


ORDER = """
stat:0.0 kv:0.0 norm:0.0 stat:1.0 q:0.0 gates:0.0 kv:1.0 norm:1.0 plan_a:0.0 s1:0.0 s1:0.1 s1:0.2 s1:0.3 q:1.0
s1:0.4 s1:0.5 s1:0.6 s1:0.7 max1:0.0 stat:2.0 stat:3.0 plan_b:0.0 plan_c:0.0 s1:1.0 s1:1.1 st1:0.0 plan_c:1.0
st1:0.1 s1:1.2 st1:0.2 st1:0.3 s1:1.3 st1:0.4 st1:0.5 s1:1.4 s1:1.5 st1:0.6 s1:1.6 st1:0.7 s1:1.7 u:0.0 pv1:0.0
pv1:0.1 max1:1.0 heads1:0.0 kv:2.0 depool:0.0 o1:0.0 st1:1.0 y1:0.0 st1:1.1 norm:2.0 stat:0.1 st1:1.2 st1:1.3
q:2.0 depool:1.0 st1:1.4 st1:1.5 norm:0.1 st1:1.6 st1:1.7 consts:0.0 pv1:1.0 route:0.0 depool:2.0 pv1:1.1
heads1:1.0 s1:2.0 s1:2.1 o1:1.0 s1:2.2 kv:3.0 y1:1.0 norm:3.0 stat:1.1 s1:2.3 q:3.0 qkv2:0.0 s1:2.4 s1:2.5
s1:2.6 norm:1.1 s1:2.7 depool:3.0 route:1.0 max1:2.0 s2:0.0 s2:0.1 s2:0.2 scale2:0.0 s2:0.3 scale2:0.1
scale2:0.2 pt2:0.0 st1:2.0 st1:2.1 pt2:0.1 pt2:0.2 st1:2.2 st1:2.3 scale2:0.3 st1:2.4 s1:3.0 pv2:0.0 st1:2.5
pt2:0.3 st1:2.6 st1:2.7 s1:3.1 pv1:2.0 pv1:2.1 pv2:0.1 heads1:2.0 s1:3.2 y2:0.0 o1:2.0 stat:0.2 s1:3.3 s1:3.4
s1:3.5 qkv2:1.0 s1:3.6 s1:3.7 y1:2.0 max1:3.0 norm:0.2 stat:2.1 s2:1.0 s2:1.1 s2:1.2 scale2:1.0 scale2:1.1
s2:1.3 pt2:1.0 pt2:1.1 scale2:1.2 st1:3.0 y3:0.0 st1:3.1 st1:3.2 pv2:1.0 norm:2.1 stat:0.3 scale2:1.3 pt2:1.2
st1:3.3 st1:3.4 route:2.0 pt2:1.3 st1:3.5 st1:3.6 st1:3.7 pv1:3.0 norm:0.3 pv2:1.1 gate:0.0 shared:0.0 y2:1.0
pv1:3.1 gate_t:0.0 wide:0.0 heads1:3.0 wide:0.1 plan_c:2.0 up:0.0 up:0.1 o1:3.0 stat:1.2 up:0.2 wide:0.2 y1:3.0
qkv2:2.0 stat:3.1 down:0.0 down:0.1 down:0.2 norm:3.1 up:0.3 norm:1.2 route:3.0 s2:2.0 wide:0.3 down:0.3 s2:2.1
s2:2.2 scale2:2.0 y3:1.0 s2:2.3 up:0.4 stat:1.3 scale2:2.1 up:0.5 scale2:2.2 pt2:2.0 up:0.6 scale2:2.3 pt2:2.1
pt2:2.2 down:0.4 pt2:2.3 up:0.7 pv2:2.0 norm:1.3 pv2:2.1 gate:1.0 qkv2:3.0 down:0.5 y2:2.0 down:0.6 plan_c:3.0
down:0.7 gate_t:1.0 s2:3.0 stat:2.2 s2:3.1 wide:1.0 s2:3.2 wide:1.1 s2:3.3 scale2:3.0 y4:0.0 up:1.0 up:1.1
norm:2.2 scale2:3.1 scale2:3.2 wide:1.2 scale2:3.3 pt2:3.0 pt2:3.1 pt2:3.2 down:1.0 up:1.2 y3:2.0 down:1.1
stat:2.3 pt2:3.3 up:1.3 down:1.2 pv2:3.0 up:1.4 norm:2.3 wide:1.3 pv2:3.1 gate:2.0 up:1.5 down:1.3 down:1.4
up:1.6 y2:3.0 stat:3.2 shared:1.0 gate_t:2.0 up:1.7 wide:2.0 down:1.5 down:1.6 wide:2.1 down:1.7 up:2.0 up:2.1
norm:3.2 down:2.0 wide:2.2 y4:1.0 y3:3.0 up:2.2 stat:3.3 down:2.1 up:2.3 up:2.4 norm:3.3 wide:2.3 down:2.2
up:2.5 gate:3.0 down:2.3 shared:2.0 down:2.4 up:2.6 shared:3.0 down:2.5 gate_t:3.0 up:2.7 wide:3.0 down:2.6
wide:3.1 down:2.7 up:3.0 up:3.1 up:3.2 wide:3.2 down:3.0 down:3.1 down:3.2 up:3.3 wide:3.3 up:3.4 up:3.5
down:3.3 down:3.4 up:3.6 down:3.5 up:3.7 down:3.6 down:3.7 y4:2.0 y4:3.0
"""


def make_schedule():
    steps = []
    for word in ORDER.split():
        what, numbers = word.split(":")
        b, i = numbers.split(".")
        steps.append((what, int(b), int(i)))
    return steps


SCHEDULE = make_schedule()
ACT_AT, DVE_AT = {}, {}
_act, _dve = 0, 0
for _step in SCHEDULE:
    assert _step not in ACT_AT
    ACT_AT[_step], DVE_AT[_step] = _act, _dve
    _act += USES[_step[0]][0]
    _dve += USES[_step[0]][1]


def order_of(name):
    return {step: n for n, step in enumerate(s for s in SCHEDULE if s[0] == name)}


STAT_AT, NORM_AT = order_of("stat"), order_of("norm")
NORMS = list(NORM_AT)
PARTS_AT = {step: n for n, step in enumerate(s for s in SCHEDULE if s[0] in ("kv", "q"))}
XN_BUFS = 4
EXPERT_BUFS = 3


def expert(k):
    return ("down", k // E, k % E)


def columns(*fields):
    at, out = 0, {}
    for name, width in fields:
        out[name] = (at, at + width)
        at += width
    return out, at


PACK_A, PACK_A_W = columns(("wk", CC * D), ("wv", CC * D), ("wq", D), ("bq", 1), ("bk", 1), ("bv", D),
                           ("mask_col", B * TT))
PACK_C, PACK_C_W = columns(("ident", P), ("tri", P), ("ones", P), ("decay", 2 * P), ("position", T),
                           ("row", 2), ("alpha", 1))
PACK_B, PACK_B_W = columns(("wo_x", D), ("wo_u", D), ("b_out", D), ("wr", NH), ("br", NH),
                           ("wo2", 2 * D), ("bo", D), ("w_in", D), ("b_in", D), ("g_res", 1), ("g_init", D),
                           ("gates", 4))
PACK_E, PACK_E_W = columns(("gate", E), ("b1", E), ("b2", E), ("sw1", HALVES * P), ("sw2", HALVES * P),
                           ("sw3", HALVES * D), ("w1", E * D), ("w3", E * D), ("w2", E * D))
GATE_ROWS = 4 * E


def flamingo(nc, x, ctx_tok, ctx_feat, pack_a, pack_b, pack_c, pack_e, mask_bc, lens,
             head_w, head_b, sel_in, b3_in, out):
    with ExitStack() as stack:
        def sb(name, shape, dt=F32):
            return stack.enter_context(nc.sbuf_tensor(name, shape, dt))

        def sem(name):
            return stack.enter_context(nc.semaphore(name))

        xs = sb("xs", [P, B * TT, D])
        x1 = sb("x1", [P, 2 * TT, D])
        x2 = sb("x2", [P, 2 * TT, D])
        x3 = sb("x3", [P, 2 * TT, D])
        resid = [xs, x1, x2, x3]
        outs = xs
        ctok = sb("ctok", [P, B * TT, DC])
        cT = sb("cT", [P, B, CC, T])
        wa = sb("wa", [P, PACK_A_W])
        wb = sb("wb", [P, PACK_B_W])
        wc = sb("wc", [P, PACK_C_W])
        we = sb("we", [P, PACK_E_W])
        maskb = sb("maskb", [P, B, T])
        lens_i = sb("lens_i", [P, TT, B], I32)

        def A(name):
            return wa[:, PACK_A[name][0]:PACK_A[name][1]]

        def W(name):
            return wb[:, PACK_B[name][0]:PACK_B[name][1]]

        def C(name):
            return wc[:, PACK_C[name][0]:PACK_C[name][1]]

        def X(name):
            return we[:, PACK_E[name][0]:PACK_E[name][1]]

        ident = C("ident")

        tg = sb("tg", [P, 4])
        gated_bias = sb("gated_bias", [P, 3, D])
        base = [sb(f"base{k}", [P, 2, TT, D]) for k in range(3)]
        w_in_g = sb("w_in_g", [P, D])
        half = sb("half", [P, TT])
        bias_row = sb("bias_row", [1, B, T], F32R)
        sel = sb("sel", [GATE_ROWS, E, P], F32R)
        b3s = sb("b3s", [GATE_ROWS, E, P], F32R)

        lens_f = sb("lens_f", [P, TT, B])
        bidx = sb("bidx", [P, TT, B])
        wrapped = sb("wrapped", [P, TT, B])
        p2 = sb("p2", [P, NA, TT, T])
        hits = p2[:, :, :, 0:T // 2].bitcast(BF16)
        pT2 = sb("pT2", [P, NA, TT, T])
        sel_f = pT2[0:GATE_ROWS, 0:2].rearrange("p a c t -> p (a c t)")
        b3_f = pT2[0:GATE_ROWS, 2:4].rearrange("p a c t -> p (a c t)")
        b3_hi = p2[0:GATE_ROWS, 0:2].rearrange("p a c t -> p (a c t)").bitcast(F32R)
        bound = sb("bound", [P, TT, B], BF16)
        counts_w = sb("counts_w", [P, 2, P], BF16)
        pick = sb("pick", [P, 2, TT, T])
        ssq = sb("ssq", [P, B * TT])
        const_rows = sb("const_rows", [1, 2, T], F32R)
        ms = sb("ms", [P, B * TT])
        rs = sb("rs", [P, B * TT])
        half8 = sb("half8", [P, B * TT])
        u = sb("u", [P, B * TT, D])
        dp = sb("dp", [P, B, TT, D])

        st = sb("st", [P, B, 4, TT, 6])
        mv = sb("mv", [P, B, 4, TT, 2])
        veps = sb("veps", [P, B, 4, TT])
        rstd = sb("rstd", [P, B, 4, TT])
        xn = sb("xn", [P, XN_BUFS, TT, D])
        xnT = [sb(f"xnT{k}", [P, 2, T]) for k in range(4)]
        xsum = sb("xsum", [P, B])

        qkf = sb("qkf", [P, 2, T])
        parts = sb("parts", [P, 2, 4, T], F32R)
        vtmp = sb("vtmp", [P, TT, D])
        v1 = sb("v1", [P, 2, TT, H1, 2, HD1])
        qstack = sb("qstack", [P, 2, PAIRS, T], F32R)
        kstack = sb("kstack", [P, 2, PAIRS, T], F32R)
        mx = sb("mx", [P, B, TT, H1])
        mxT = sb("mxT", [H1, 2, T], F32R)
        pT1 = sb("pT1", [P, H1, TT, T])
        rec1 = sb("rec1", [P, B, TT, H1])
        oS = sb("oS", [P, 2, T])
        o1 = sb("o1", [P, TT, D])
        oT1 = sb("oT1", [P, T])

        rt = sb("rt", [1, B, NH])
        top = sb("top", [1, B, 8])
        topi = sb("topi", [1, B, 8], U32)
        negi = sb("negi", [1, B, 8])
        sorti = sb("sorti", [1, B, 8])
        heads = sb("heads", [1, B, 8], I32)
        w2h = sb("w2h", [P, 2, 3, NA * HD2])
        b2h = sb("b2h", [P, B, 2, 3])
        bq8 = sb("bq8", [P, B, 2])
        q2 = sb("q2", [P, 2, T])
        k2 = sb("k2", [P, 2, T])
        v2 = sb("v2", [P, TT, NA * HD2])
        nm2 = sb("nm2", [P, B, NA, TT])
        sum2 = sb("sum2", [P, B, NA, TT])
        rec2 = sb("rec2", [P, B, NA, TT])
        oT2 = sb("oT2", [P, 2, T])

        lg = sb("lg", [P, B, TT, E])
        gtop = sb("gtop", [P, B, TT, 8])
        gidx = sb("gidx", [P, B, TT, 8], U32)
        gidf = sb("gidf", [P, B, TT, 2])
        nmax = sb("nmax", [P, B, TT])
        gexp = sb("gexp", [P, B, TT, E])
        gsum = sb("gsum", [P, B, TT])
        grec = sb("grec", [P, B, TT])
        m1 = sb("m1", [P, B, TT, E])
        wsel = sb("wsel", [P, B, TT, E])
        whi = sb("whi", [P, B, TT, E], F32R)
        gpack = sb("gpack", [P, B, TT, GATE_ROWS])
        gT = sb("gT", [GATE_ROWS, B, T], F32R)
        xw = sb("xw", [P, 2, 2, T])
        sq_junk = xw[:, 0]
        hx = sb("hx", [P, EXPERT_BUFS, 2, T])
        prod = cT[:, 0:2].rearrange("p b c t -> p (b c) t")
        gs = ctok[:, 0:4, :].rearrange("p (b c) t -> p b c t", b=2)
        sg = ctok[:, 4:6, :]
        yT = ctok[:, 6:8, :]

        act_banks = [stack.enter_context(nc.psum_tensor(f"act_bank{i}", [P, 512], F32)) for i in range(ACT_RING)]
        dve_banks = [stack.enter_context(nc.psum_tensor(f"dve_bank{i}", [P, 512], F32)) for i in range(DVE_RING)]

        def abank(n):
            return act_banks[n % ACT_RING]

        def dbank(n):
            return dve_banks[n % DVE_RING]

        act_full, act_done = sem("act_full"), sem("act_done")
        dve_full, dve_done = sem("dve_full"), sem("dve_done")
        x_in = [sem(f"x_in{b}") for b in range(B)]
        cT_in = [sem(f"cT_in{b}") for b in range(B)]
        ctok_in = sem("ctok_in")
        mask_in, masks_in = sem("mask_in"), sem("masks_in")
        p2_scaled = sem("p2_scaled")
        wa_in, wb_in, wc_in, we_in = sem("wa_in"), sem("wb_in"), sem("wc_in"), sem("we_in")
        lens_in, gate_rows_in, lens_cast = sem("lens_in"), sem("gate_rows_in"), sem("lens_cast")
        tanh_done = sem("tanh_done")
        base_done = [sem(f"base_done{k}") for k in range(3)]
        rows_made = sem("rows_made")
        consts_made = sem("consts_made")
        stats_done = sem("stats_done")
        rstd_done = sem("rstd_done")
        xn_done = sem("xn_done")
        parts_done = sem("parts_done")
        const_rows_in = sem("const_rows_in")
        mask_rows_in = [sem(f"mask_rows_in{b}") for b in range(B)]
        stack_in = [sem(f"stack_in{b}") for b in range(B)]
        max_in = [sem(f"max_in{b}") for b in range(B)]
        v1_done = sem("v1_done")
        v_ones = sem("v_ones")
        heads_done = sem("heads_done")
        head_in = [sem(f"head_in{b}") for b in range(B)]
        bq8_done = sem("bq8_done")
        nm2_done = sem("nm2_done")
        gate_max_done, gate_exp_done, gpack_done = sem("gate_max_done"), sem("gate_exp_done"), sem("gpack_done")
        ssq_done, rs_done, u_done = sem("ssq_done"), sem("rs_done"), sem("u_done")
        hits_done = sem("hits_done")
        up_read = sem("up_read")
        prod_read = sem("prod_read")
        dve_chain, pool_chain = sem("dve_chain"), sem("pool_chain")
        out_done = [sem(f"out_done{b}") for b in range(B)]

        block = stack.enter_context(nc.Block())

        def tiles(t, b):
            return t[:, b * TT:(b + 1) * TT, :]

        def x_of(k, b):
            return tiles(resid[k], b if k == 0 else b % 2)

        @block.sync
        def _(sp):
            def load_batch(b):
                sp.dma_start(tiles(xs, b), x.rearrange("b (t p) d -> p (b t) d", p=P)[:, b * TT:(b + 1) * TT, :]
                             ).then_inc(x_in[b], 16)
                sp.dma_start(cT[:, b], ctx_feat.rearrange("(c p) (b t) -> p b c t", p=P, b=B)[:, b]
                             ).then_inc(cT_in[b], 16)

            load_batch(0)
            sp.wait_ge(rows_made, 1)
            for j in range(2):
                for n, (dst, at) in enumerate(((qstack, ROW_BIAS), (kstack, ROW_MAX))):
                    row = const_rows[0:1, n:n + 1, :].to_broadcast([1, 2 * PAIRS, T]).bitcast(F32)
                    sp.dma_start(dst[64 * j + at:64 * j + at + 1].rearrange("r b n t -> r (b n) t").bitcast(F32), row
                                 ).then_inc(const_rows_in, 16)
            load_batch(1)

            def mask_rows(b):
                for j in range(2):
                    r = 64 * j + ROW_BIAS
                    sp.dma_start(kstack[r:r + 1, b % 2].bitcast(F32),
                                 bias_row[0:1, b:b + 1, :].to_broadcast([1, PAIRS, T]).bitcast(F32)
                                 ).then_inc(mask_rows_in[b], 16)

            def restack(step, dst, sources):
                b = step[1]
                sp.wait_ge(parts_done, PARTS_AT[step] + 1)
                for r, s in enumerate(sources):
                    for j in range(2):
                        lo = 64 * j + HD1 * r
                        sp.dma_start(dst[lo:lo + HD1, b % 2].bitcast(F32),
                                     parts[64 * j:64 * j + 64, b % 2, s, :].bitcast(F32)).then_inc(stack_in[b], 16)

            def fetch_heads(b):
                if b >= 2:
                    sp.wait_ge(act_done, ACT_AT[("qkv2", b - 2, 0)] + 3)
                sp.wait_ge(heads_done, b + 1)
                for a in range(NA):
                    h = sp.value_load(heads[0:1, b, a:a + 1], min_val=0, max_val=NH - 1)
                    sp.dma_start(w2h[:, b % 2, :, a * HD2:(a + 1) * HD2],
                                 head_w[bass.ds(h, 1)].rearrange("h p (m d) -> (h p) m d", m=3)).then_inc(head_in[b], 16)
                    lo = HD2 * (a % 2)
                    sp.dma_start(b2h[lo:lo + HD2, b, a // 2, :],
                                 head_b[bass.ds(h, 1)].rearrange("h p m -> (h p) m")).then_inc(head_in[b], 16)

            for step in SCHEDULE:
                what, b, i = step
                if what == "kv":
                    if b >= 2:
                        sp.wait_ge(act_done, ACT_AT[("st1", b - 2, H1 - 1)] + 1)
                    restack(step, kstack, (2, 2, 3))
                    sp.wait_ge(rows_made, b + 2)
                    mask_rows(b)
                elif what == "q":
                    restack(step, qstack, (0, 1, 0))
                    if b == 0:
                        load_batch(2)
                        load_batch(3)
                elif what == "route":
                    fetch_heads(b)
                elif what == "y4":
                    sp.wait_ge(dve_done, DVE_AT[step] + 1)
                    sp.dma_start(out.rearrange("b (t p) d -> p (b t) d", p=P)[:, b * TT:(b + 1) * TT, :],
                                 tiles(outs, b)).then_inc(out_done[b], 16)
            for b in range(B):
                sp.wait_ge(out_done[b], 16)

        @block.tensor
        def _(pe):
            def take_act(n):
                if n >= ACT_RING:
                    pe.wait_ge(act_done, n - ACT_RING + 1)
                return abank(n)

            def take_dve(n):
                if n >= DVE_RING:
                    pe.wait_ge(dve_done, n - DVE_RING + 1)
                return dbank(n)

            for step in SCHEDULE:
                what, b, i = step
                na, nd = ACT_AT[step], DVE_AT[step]
                if what == "kv":
                    if b == 0:
                        pe.wait_ge(wa_in, 16)
                    pe.wait_ge(cT_in[b], 16)
                    bank = take_dve(nd)
                    for c in range(CC):
                        mm = pe.matmul(bank[:, 0:T], A("wk")[:, c * D:(c + 1) * D], cT[:, b, c, :],
                                       start=(c == 0), stop=(c == CC - 1))
                    mm.then_inc(dve_full, 1)
                    bank = take_dve(nd + 1)
                    for t in range(TT):
                        for c in range(CC):
                            mm = pe.matmul(bank[:, t * D:(t + 1) * D], cT[:, b, c, t * P:(t + 1) * P],
                                           A("wv")[:, c * D:(c + 1) * D], start=(c == 0), stop=(c == CC - 1))
                    mm.then_inc(dve_full, 1)
                elif what == "norm":
                    if b == 0 and i == 0:
                        pe.wait_ge(wc_in, 16)
                    pe.wait_ge(xn_done, NORM_AT[step] + 1)
                    bank = take_act(na)
                    for t in range(TT):
                        mm = pe.transpose(bank[:, t * P:(t + 1) * P], xn[:, NORM_AT[step] % XN_BUFS, t, :], ident)
                    mm.then_inc(act_full, 1)
                elif what == "q":
                    pe.wait_ge(act_done, ACT_AT[("norm", b, 0)] + 1)
                    bank = take_dve(nd)
                    pe.matmul(bank[:, 0:T], A("wq"), xnT[0][:, b % 2, :], start=True, stop=True).then_inc(dve_full, 1)
                elif what == "plan_a":
                    bank = take_dve(nd)
                    pe.wait_ge(lens_cast, 1)
                    pe.matmul(bank[:, 0:B], C("tri"), lens_f[:, 0, :], start=True, stop=True)
                    pe.matmul(bank[:, B:2 * B], C("ones"), lens_f[:, 0, :], start=True, stop=False)
                    pe.matmul(bank[:, B:2 * B], C("tri"), lens_f[:, 1, :], start=False, stop=True
                              ).then_inc(dve_full, 1)
                elif what == "plan_b":
                    bank = take_dve(nd)
                    pe.wait_ge(hits_done, 1)
                    for bb in range(B):
                        for t in range(TT):
                            for c in range(TT):
                                mm = pe.matmul(bank[:, t * B + bb:t * B + bb + 1], hits[:, bb, c, t * P:(t + 1) * P],
                                               counts_w[:, 1, 0:1], start=(c == 0), stop=(c == TT - 1))
                    mm.then_inc(dve_full, 1)
                elif what == "plan_c":
                    pe.wait_ge(dve_done, DVE_AT[("plan_b", 0, 0)] + 1)
                    bank = take_dve(nd)
                    for t in range(TT):
                        for c in range(t + 1):
                            mm = pe.matmul(bank[:, t * P:(t + 1) * P],
                                           bound[:, c, b:b + 1].to_broadcast([P, P]),
                                           counts_w[:, 0 if c == t else 1, :], start=(c == 0), stop=(c == t))
                    mm.then_inc(dve_full, 1)
                elif what == "depool":
                    pe.wait_ge(u_done, 1)
                    bank = take_act(na)
                    pe.matmul(bank[:, 0:D], C("decay")[:, 0:P], u[:, b * TT, :], start=True, stop=True)
                    pe.matmul(bank[:, D:2 * D], C("decay")[:, P:2 * P], u[:, b * TT, :], start=True, stop=False)
                    pe.matmul(bank[:, D:2 * D], C("decay")[:, 0:P], u[:, b * TT + 1, :], start=False, stop=True
                              ).then_inc(act_full, 1)
                elif what == "s1":
                    j, pair = divmod(i, PAIRS)
                    if i == 0:
                        pe.wait_ge(const_rows_in, 4 * 16)
                        pe.wait_ge(mask_rows_in[b], 2 * 16)
                        pe.wait_ge(stack_in[b], 12 * 16)
                    bank = take_dve(nd)
                    lo, hi = 64 * j, 64 * j + ROW_MAX
                    for t in range(TT):
                        mm = pe.matmul(bank[:, t * T:(t + 1) * T], qstack[lo:hi, b % 2, pair, t * P:(t + 1) * P],
                                       kstack[lo:hi, b % 2, pair, :], start=True, stop=True)
                    mm.then_inc(dve_full, 1)
                elif what == "max1":
                    pe.wait_ge(dve_done, DVE_AT[("s1", b, H1 - 1)] + 1)
                    bank = take_act(na)
                    for t in range(TT):
                        mm = pe.transpose(bank[0:H1, t * P:(t + 1) * P], mx[:, b, t, :], ident)
                    mm.then_inc(act_full, 1)
                elif what == "st1":
                    j, pair = divmod(i, PAIRS)
                    if i == 0:
                        pe.wait_ge(max_in[b], 2 * 16)
                    bank = take_act(na)
                    lo, hi = 64 * j, 64 * j + ROW_MAX + 1
                    for c in range(TT):
                        mm = pe.matmul(bank[:, c * T:(c + 1) * T], kstack[lo:hi, b % 2, pair, c * P:(c + 1) * P],
                                       qstack[lo:hi, b % 2, pair, :], start=True, stop=True)
                    mm.then_inc(act_full, 1)
                elif what == "pv1":
                    pe.wait_ge(v1_done, b + 1)
                    bank = take_act(na)
                    pe.wait_ge(act_done, ACT_AT[("st1", b, 4 * i + 3)] + 1)
                    for c in range(TT):
                        for h in range(4 * i, 4 * i + 4):
                            lo = 2 * HD1 * (h % 4)
                            mm = pe.matmul(bank[lo:lo + 2 * HD1, 0:T],
                                           v1[:, b % 2, c, h].rearrange("p k d -> p (k d)"), pT1[:, h, c, :],
                                           start=(c == 0), stop=(c == TT - 1), tile_position=(0, lo))
                    mm.then_inc(act_full, 1)
                elif what == "heads1":
                    pe.wait_ge(act_done, ACT_AT[("pv1", b, 1)] + 1)
                    bank = take_dve(nd)
                    for t in range(TT):
                        for g in range(2):
                            mm = pe.transpose(bank[:, t * T + g * P:t * T + (g + 1) * P],
                                              oS[:, g, t * P:(t + 1) * P], ident)
                    mm.then_inc(dve_full, 1)
                elif what == "o1":
                    pe.wait_ge(dve_done, DVE_AT[("heads1", b, 0)] + 1)
                    bank = take_act(na)
                    for t in range(TT):
                        mm = pe.transpose(bank[:, t * P:(t + 1) * P], o1[:, t, :], ident)
                    mm.then_inc(act_full, 1)
                elif what == "y1":
                    if b == 0:
                        pe.wait_ge(wb_in, 16)
                    bank = take_dve(nd)
                    pe.wait_ge(act_done, ACT_AT[("o1", b, 0)] + 1)
                    for t in range(TT):
                        pe.matmul(bank[:, t * D:(t + 1) * D], xnT[0][:, b % 2, t * P:(t + 1) * P], W("wo_x"),
                                  start=True, stop=False)
                        mm = pe.matmul(bank[:, t * D:(t + 1) * D], oT1[:, t * P:(t + 1) * P], W("wo_u"),
                                       start=False, stop=True)
                    mm.then_inc(dve_full, 1)
                elif what == "route":
                    pe.wait_ge(act_done, ACT_AT[("norm", b, 1)] + 1)
                    bank = take_dve(nd)
                    pe.matmul(bank[0:1, 0:NH], xsum[:, b:b + 1], W("wr"), start=True, stop=True
                              ).then_inc(dve_full, 1)
                elif what == "qkv2":
                    pe.wait_ge(head_in[b], 8 * 16)
                    for m in range(2):
                        bank = take_act(na + m)
                        for g in range(2):
                            mm = pe.matmul(bank[:, g * T:(g + 1) * T],
                                           w2h[:, b % 2, m, g * P:(g + 1) * P], xnT[1][:, b % 2, :],
                                           start=True, stop=True)
                        mm.then_inc(act_full, 1)
                    bank = take_act(na + 2)
                    for t in range(TT):
                        mm = pe.matmul(bank[:, t * NA * HD2:(t + 1) * NA * HD2], xnT[1][:, b % 2, t * P:(t + 1) * P],
                                       w2h[:, b % 2, 2, :], start=True, stop=True)
                    mm.then_inc(act_full, 1)
                elif what == "s2":
                    if i == 0:
                        pe.wait_ge(act_done, ACT_AT[("qkv2", b, 0)] + 2)
                    bank = take_act(na)
                    lo, g = HD2 * (i % 2), i // 2
                    for t in range(TT):
                        mm = pe.matmul(bank[:, t * T:(t + 1) * T], q2[lo:lo + HD2, g, t * P:(t + 1) * P],
                                       k2[lo:lo + HD2, g, :], start=True, stop=True)
                    mm.then_inc(act_full, 1)
                elif what == "pt2":
                    pe.wait_ge(p2_scaled, NA * b + i + 1)
                    bank = take_dve(nd)
                    for c in range(TT):
                        for t in range(TT):
                            mm = pe.transpose(bank[:, c * T + t * P:c * T + (t + 1) * P],
                                              p2[:, i, t, c * P:(c + 1) * P], ident)
                    mm.then_inc(dve_full, 1)
                elif what == "pv2":
                    pe.wait_ge(act_done, ACT_AT[("qkv2", b, 0)] + 3)
                    bank = take_act(na)
                    pe.wait_ge(dve_done, DVE_AT[("pt2", b, 2 * i + 1)] + 1)
                    for c in range(TT):
                        for a in (2 * i, 2 * i + 1):
                            lo = HD2 * (a % 2)
                            mm = pe.matmul(bank[lo:lo + HD2, 0:T], v2[:, c, a * HD2:(a + 1) * HD2], pT2[:, a, c, :],
                                           start=(c == 0), stop=(c == TT - 1), tile_position=(0, lo))
                    mm.then_inc(act_full, 1)
                elif what == "y2":
                    pe.wait_ge(act_done, ACT_AT[("pv2", b, 1)] + 1)
                    bank = take_dve(nd)
                    for t in range(TT):
                        for g in range(2):
                            mm = pe.matmul(bank[:, t * D:(t + 1) * D], oT2[:, g, t * P:(t + 1) * P],
                                           W("wo2")[:, g * D:(g + 1) * D], start=(g == 0), stop=(g == 1))
                    mm.then_inc(dve_full, 1)
                elif what == "y3":
                    if b == 0:
                        pe.wait_ge(consts_made, 1)
                    pe.wait_ge(act_done, max(ACT_AT[("norm", b, 2)], ACT_AT[("depool", b, 0)]) + 1)
                    pe.wait_ge(dve_done, DVE_AT[("plan_c", b, 0)] + 1)
                    bank = take_dve(nd)
                    for t in range(TT):
                        pe.matmul(bank[:, t * D:(t + 1) * D], xnT[2][:, b % 2, t * P:(t + 1) * P], w_in_g[:],
                                  start=True, stop=False)
                        for c in range(TT):
                            mm = pe.matmul(bank[:, t * D:(t + 1) * D], pick[:, b % 2, c, t * P:(t + 1) * P],
                                           dp[:, b, c, :], start=False, stop=(c == TT - 1))
                    mm.then_inc(dve_full, 1)
                elif what == "gate":
                    if b == 0:
                        pe.wait_ge(we_in, 16)
                    pe.wait_ge(act_done, ACT_AT[("norm", b, 3)] + 1)
                    bank = take_dve(nd)
                    for t in range(TT):
                        mm = pe.matmul(bank[:, t * E:(t + 1) * E], xnT[3][:, b % 2, t * P:(t + 1) * P], X("gate"),
                                       start=True, stop=True)
                    mm.then_inc(dve_full, 1)
                elif what == "gate_t":
                    pe.wait_ge(gpack_done, b + 1)
                    bank = take_act(na)
                    for t in range(TT):
                        mm = pe.transpose(bank[0:GATE_ROWS, t * P:(t + 1) * P], gpack[:, b, t, :], ident)
                    mm.then_inc(act_full, 1)
                elif what == "wide":
                    if i == 0:
                        if b == 0:
                            pe.wait_ge(consts_made, 3)
                        pe.wait_ge(act_done, ACT_AT[("gate_t", b, 0)] + 1)
                    bank = take_dve(nd)
                    for e in range(2):
                        mm = pe.matmul(bank[:, e * T:(e + 1) * T], sel[:, 2 * i + e, :], gT[:, b, :],
                                       start=True, stop=True)
                    mm.then_inc(dve_full, 1)
                elif what == "up":
                    bank = take_act(na)
                    pe.wait_ge(dve_done, DVE_AT[("wide", b, i // 2)] + 1)
                    xe = xw[:, i // 2 % 2, i % 2, :]
                    pe.matmul(bank[:, 0:T], X("w1")[:, i * D:(i + 1) * D], xe, start=True, stop=True)
                    pe.matmul(bank[:, T:2 * T], X("w3")[:, i * D:(i + 1) * D], xe, start=True, stop=False
                              ).then_inc(up_read, 1)
                    pe.matmul(bank[:, T:2 * T], b3s[:, i, :], gT[:, b, :], start=False, stop=True
                              ).then_inc(act_full, 1)
                elif what == "down":
                    pe.wait_ge(act_done, ACT_AT[("up", b, i)] + 1)
                    bank = take_dve(nd)
                    pe.matmul(bank[:, 0:T], X("w2")[:, i * D:(i + 1) * D], hx[:, (b * E + i) % EXPERT_BUFS, 0, :],
                              start=True, stop=True).then_inc(dve_full, 1)
                elif what == "shared":
                    for m, (name, bank) in enumerate((("sw1", take_act(na)), ("sw2", take_dve(nd)))):
                        for c in range(HALVES):
                            mm = pe.matmul(bank[:, c * T:(c + 1) * T], X(name)[:, c * P:(c + 1) * P], xnT[3][:, b % 2, :],
                                           start=True, stop=True)
                        mm.then_inc((act_full, dve_full)[m], 1)
                elif what == "y4":
                    bank = take_dve(nd)
                    pe.wait_ge(dve_done, DVE_AT[("shared", b, 0)] + 1)
                    pe.wait_ge(prod_read, E * (b + 1))
                    for t in range(TT):
                        for c in range(HALVES):
                            pe.matmul(bank[:, t * D:(t + 1) * D], gs[:, b % 2, c, t * P:(t + 1) * P],
                                      X("sw3")[:, c * D:(c + 1) * D], start=(c == 0), stop=False)
                        mm = pe.matmul(bank[:, t * D:(t + 1) * D], yT[:, b % 2, t * P:(t + 1) * P], ident,
                                       start=False, stop=True)
                    mm.then_inc(dve_full, 1)

        @block.scalar
        def _(act):
            act.dma_start(wa[:], pack_a).then_inc(wa_in, 16)
            masks = mask_bc.rearrange("p (b t) -> p b t", b=B)
            act.dma_start(maskb[:, 0], masks[:, 0]).then_inc(mask_in, 16)
            act.dma_start(lens_i[:], lens.rearrange("p (t b) -> p t b", b=B)).then_inc(lens_in, 16)
            act.dma_start(wc[:], pack_c).then_inc(wc_in, 16)
            act.dma_start(wb[:], pack_b).then_inc(wb_in, 16)
            act.dma_start(maskb[:, 1:], masks[:, 1:]).then_inc(masks_in, 16)
            for step in SCHEDULE:
                what, b, i = step
                n = ACT_AT[step]
                bank = abank(n)
                if USES[what][0] and what not in ("qkv2",):
                    act.wait_ge(act_full, n + 1)
                if what == "gates":
                    act.wait_ge(wb_in, 16)
                    act.activation(tg[:], W("gates"), ACT.Tanh).then_inc(tanh_done, 1)
                elif what == "u":
                    act.wait_ge(ctok_in, 16)
                    for m in range(B * TT):
                        if m >= 2:
                            act.wait_ge(ssq_done, m - 1)
                        act.activation(sq_junk[:, m % 2, :], ctok[:, m, :], ACT.Square, accum_out=ssq[:, m:m + 1]
                                       ).then_inc(ssq_done, 1)
                elif what == "norm":
                    if i == 1:
                        act.activation(xnT[1][:, b % 2, :], bank[:, 0:T], ACT.Identity, accum_out=xsum[:, b:b + 1]
                                       ).then_inc(act_done, 1)
                    else:
                        act.copy(xnT[i][:, b % 2, :], bank[:, 0:T]).then_inc(act_done, 1)
                elif what == "depool":
                    act.copy(dp[:, b].rearrange("p c d -> p (c d)"), bank[:, 0:TT * D]).then_inc(act_done, 1)
                elif what == "max1":
                    act.copy(mxT[:, b % 2, :], bank[0:H1, 0:T]).then_inc(act_done, 1)
                    act.wait_ge(act_done, n + 1)
                    for j in range(2):
                        r = 64 * j + ROW_MAX
                        act.dma_start(qstack[r:r + 1, b % 2].bitcast(F32),
                                      mxT[PAIRS * j:PAIRS * (j + 1), b % 2, :].bitcast(F32)).then_inc(max_in[b], 16)
                    if b == 0:
                        act.dma_start(ctok[:], ctx_tok.rearrange("b (t p) d -> p (b t) d", p=P)
                                      ).then_inc(ctok_in, 16)
                        act.dma_start(sel_f, sel_in).then_inc(gate_rows_in, 16)
                        act.dma_start(b3_f, b3_in).then_inc(gate_rows_in, 16)
                        act.dma_start(we[:], pack_e).then_inc(we_in, 16)
                elif what == "st1":
                    if b >= 1:
                        act.wait_ge(act_full, ACT_AT[("pv1", b - 1, i // 4)] + 1)
                    act.activation(pT1[:, i].rearrange("p c t -> p (c t)"), bank[:], ACT.Exp, scale=HD1 ** -0.5).then_inc(act_done, 1)
                elif what == "pv1":
                    act.copy(oS[:, i, :], bank[:, 0:T]).then_inc(act_done, 1)
                elif what == "o1":
                    act.copy(oT1[:], bank[:, 0:T]).then_inc(act_done, 1)
                elif what == "qkv2":
                    act.wait_ge(head_in[b], 8 * 16)
                    act.activation(bq8[:, b, :], b2h[:, b, :, 0], ACT.Identity, scale=HD2 ** -0.5).then_inc(bq8_done, 1)
                    act.wait_ge(bq8_done, b + 1)
                    act.wait_ge(act_full, n + 1)
                    for g in range(2):
                        ins = act.activation(q2[:, g, :], abank(n)[:, g * T:(g + 1) * T], ACT.Identity,
                                             scale=HD2 ** -0.5, bias=bq8[:, b, g:g + 1])
                    ins.then_inc(act_done, 1)
                    act.wait_ge(act_full, n + 2)
                    for g in range(2):
                        ins = act.activation(k2[:, g, :], abank(n + 1)[:, g * T:(g + 1) * T], ACT.Identity,
                                             bias=b2h[:, b, g, 1:2])
                    ins.then_inc(act_done, 1)
                    act.wait_ge(act_full, n + 3)
                    act.copy(v2[:].rearrange("p t d -> p (t d)"), abank(n + 2)[:]).then_inc(act_done, 1)
                elif what == "s2":
                    act.wait_ge(nm2_done, NA * b + i + 1)
                    if b >= 1:
                        act.wait_ge(dve_done, DVE_AT[("pt2", b - 1, i)] + 1)
                    for t in range(TT):
                        ins = act.activation(p2[:, i, t, :], bank[:, t * T:(t + 1) * T], ACT.Exp,
                                             bias=nm2[:, b, i, t:t + 1], accum_out=sum2[:, b, i, t:t + 1])
                    ins.then_inc(act_done, 1)
                elif what == "pv2":
                    act.activation(oT2[:, i, :], bank[:, 0:T], ACT.Identity, bias=b2h[:, b, i, 2:3]
                                   ).then_inc(act_done, 1)
                elif what == "gate":
                    act.wait_ge(gate_max_done, b + 1)
                    for t in range(TT):
                        ins = act.activation(gexp[:, b, t, :], lg[:, b, t, :], ACT.Exp, bias=nmax[:, b, t:t + 1],
                                             accum_out=gsum[:, b, t:t + 1])
                    ins.then_inc(gate_exp_done, 1)
                elif what == "gate_t":
                    act.copy(gT[:, b, :], bank[0:GATE_ROWS, 0:T]).then_inc(act_done, 1)
                elif what == "up":
                    k = b * E + i
                    if k >= EXPERT_BUFS:
                        act.wait_ge(dve_done, DVE_AT[expert(k - EXPERT_BUFS)] + 1)
                    act.activation(hx[:, k % EXPERT_BUFS, 0, :], bank[:, 0:T], ACT.Silu, bias=X("b1")[:, i:i + 1])
                    act.copy(hx[:, k % EXPERT_BUFS, 1, :], bank[:, T:2 * T]).then_inc(act_done, 1)
                elif what == "shared":
                    if b >= 1:
                        act.wait_ge(dve_done, DVE_AT[("shared", b - 1, 0)] + 1)
                    act.activation(sg.rearrange("p c t -> p (c t)"), bank[:], ACT.Silu).then_inc(act_done, 1)

        @block.vector
        def _(dve):
            chained = [0]

            def link(ins):
                chained[0] += 1
                ins.then_inc(dve_chain, 1)
                dve.wait_ge(dve_chain, chained[0])

            link(dve.memset(negi[:], -100.0))
            dve.memset(v1[:], 1.0).then_inc(v_ones, 1)
            link(dve.memset(qkf[:, 0, :], 1.0))
            link(dve.tensor_copy(const_rows[0:1, 0, :], qkf[0:1, 0, :]))
            dve.tensor_scalar(const_rows[0:1, 1, :], qkf[0:1, 0, :], -1.0, None, ALU.mult).then_inc(rows_made, 1)
            dve.tensor_copy(counts_w[:, 1, :], qkf[:, 0, 0:P])

            def make_gate_rows():
                dve.wait_ge(gate_rows_in, 32)
                dve.tensor_copy(sel[:].rearrange("p e n -> p (e n)"), sel_f).then_inc(consts_made, 1)
                link(dve.tensor_copy(b3_hi, b3_f))
                dve.scalar_tensor_tensor(out=b3s[:].rearrange("p e n -> p (e n)"), in0=b3_hi.bitcast(F32),
                                         scalar=C("alpha")[0:GATE_ROWS, :], in1=b3_f, op0=ALU.mult, op1=ALU.add
                                         ).then_inc(consts_made, 1)

            def split(step, k):
                b = step[1]
                if b >= 2:
                    dve.wait_ge(stack_in[b - 2], 12 * 16)
                link(dve.tensor_copy(parts[:, b % 2, 2 * k, :], qkf[:, k, :]))
                dve.tensor_tensor(parts[:, b % 2, 2 * k + 1, :], qkf[:, k, :], parts[:, b % 2, 2 * k, :].bitcast(F32),
                                  ALU.subtract).then_inc(parts_done, 1)
                dve.wait_ge(parts_done, PARTS_AT[step] + 1)

            def project(step, k, name, n):
                dve.wait_ge(dve_full, n + 1)
                dve.scalar_tensor_tensor(out=qkf[:, k, :], in0=dbank(n)[:, 0:T], scalar=A(name),
                                         in1=maskb[:, step[1], :], op0=ALU.add, op1=ALU.mult).then_inc(dve_done, 1)
                dve.wait_ge(dve_done, n + 1)
                split(step, k)

            def residual(k, b, bank, done):
                if k < 3:
                    dve.wait_ge(base_done[k], b + 1)
                before = base[k][:, b % 2] if k < 3 else x_of(3, b)
                if k == 2 and b >= 2:
                    dve.wait_ge(dve_done, DVE_AT[("y4", b - 2, 0)] + 1)
                if k < 2 and b >= 2:
                    dve.wait_ge(base_done[k + 1], b - 1)
                after = x_of(k + 1, b) if k < 3 else tiles(outs, b)
                dve.scalar_tensor_tensor(out=after, in0=bank[:, 0:TT * D].rearrange("p (t d) -> p t d", t=TT),
                                         scalar=tg[:, k:k + 1], in1=before, op0=ALU.mult, op1=ALU.add
                                         ).then_inc(dve_done, 1)

            for step in SCHEDULE:
                what, b, i = step
                n = DVE_AT[step]
                bank = dbank(n)
                if USES[what][1] and what not in ("kv", "q", "plan_a"):
                    dve.wait_ge(dve_full, n + 1)
                if what == "stat":
                    if i == 0:
                        dve.wait_ge(x_in[b], 16)
                    else:
                        dve.wait_ge(dve_done, DVE_AT[(f"y{i}", b, 0)] + 1)
                    for t in range(TT):
                        ins = dve.bn_stats(st[:, b, i, t, :], x_of(i, b)[:, t, :])
                    link(ins)
                    for t in range(TT):
                        ins = dve.bn_aggr(mv[:, b, i, t, :], st[:, b, i, t, :])
                    ins.then_inc(stats_done, 1)
                elif what == "norm":
                    k = NORM_AT[step]
                    dve.wait_ge(rstd_done, STAT_AT[("stat", b, i)] + 1)
                    if k >= XN_BUFS:
                        dve.wait_ge(act_done, ACT_AT[NORMS[k - XN_BUFS]] + 1)
                    for t in range(TT):
                        ins = dve.tensor_scalar(xn[:, k % XN_BUFS, t, :], x_of(i, b)[:, t, :],
                                                mv[:, b, i, t, 0:1], rstd[:, b, i, t:t + 1],
                                                ALU.subtract, ALU.mult)
                    ins.then_inc(xn_done, 1)
                elif what == "kv":
                    if b == 0:
                        dve.wait_ge(wa_in, 16)
                        dve.wait_ge(mask_in, 16)
                    if b == 1:
                        dve.wait_ge(masks_in, 16)
                    dve.tensor_scalar(bias_row[:, b], maskb[0:1, b], 0.0, MASKED,
                                      ALU.is_equal, ALU.mult).then_inc(rows_made, 1)
                    project(step, 1, "bk", n)
                    dve.wait_ge(dve_full, n + 2)
                    if b >= 1:
                        dve.wait_ge(v1_done, b)
                    dve.tensor_tensor(vtmp[:], dbank(n + 1)[:, 0:TT * D].rearrange("p (t d) -> p t d", t=TT),
                                      A("bv").unsqueeze(1).to_broadcast([P, TT, D]), ALU.add).then_inc(dve_done, 1)
                elif what == "q":
                    project(step, 0, "bq", n)
                elif what == "plan_a":
                    dve.wait_ge(lens_in, 16)
                    dve.tensor_copy(lens_f[:], lens_i[:]).then_inc(lens_cast, 1)
                    dve.wait_ge(wc_in, 16)
                    dve.tensor_copy(counts_w[:, 0, :], C("tri"))
                    dve.wait_ge(dve_full, n + 1)
                    dve.tensor_scalar(bidx[:].rearrange("p t b -> p (t b)"), bank[:, 0:TT * B], -1.0, None,
                                      ALU.add).then_inc(dve_done, 1)
                    dve.wait_ge(dve_done, n + 1)
                    link(dve.tensor_scalar(wrapped[:], bidx[:], 0.0, float(T), ALU.is_lt, ALU.mult))
                    link(dve.tensor_tensor(wrapped[:], bidx[:], wrapped[:], ALU.add))
                    for bb in range(B):
                        for c in range(TT):
                            ins = dve.tensor_scalar(hits[:, bb, c, :], C("position"), wrapped[:, c, bb:bb + 1], None,
                                                    ALU.is_equal)
                    ins.then_inc(hits_done, 1)
                elif what == "plan_b":
                    dve.tensor_scalar(bound[:].rearrange("p t b -> p (t b)"), bank[:, 0:TT * B], 1.0, None,
                                      ALU.min).then_inc(dve_done, 1)
                elif what == "plan_c":
                    for c in range(TT):
                        ins = dve.tensor_scalar(pick[:, b % 2, c, :], bank[:, 0:T], 1.0, C("row")[:, c:c + 1],
                                                ALU.max, ALU.is_equal)
                    ins.then_inc(dve_done, 1)
                elif what == "u":
                    dve.wait_ge(rs_done, 1)
                    for m in range(B * TT):
                        ins = dve.scalar_tensor_tensor(out=u[:, m, :], in0=ctok[:, m, 0:D], scalar=rs[:, m:m + 1],
                                                       in1=W("g_init"), op0=ALU.mult, op1=ALU.mult)
                    ins.then_inc(u_done, 1)
                elif what == "consts":
                    dve.wait_ge(wb_in, 16)
                    dve.tensor_scalar(w_in_g[:], W("w_in"), W("g_res"), None, ALU.mult).then_inc(consts_made, 1)
                    make_gate_rows()
                elif what == "s1":
                    dve.tensor_reduce(mx[:, b, :, i], bank[:].rearrange("p (t s) -> p t s", t=TT), AX.X, ALU.max
                                      ).then_inc(dve_done, 1)
                elif what == "heads1":
                    heads_out = bank[:].rearrange("p (t h k d) -> p t h k d", t=TT, h=H1, k=2)
                    link(dve.reciprocal(rec1[:, b], heads_out[:, :, :, 1, 0]))
                    dve.tensor_tensor(o1[:].rearrange("p t (h d) -> p t h d", h=H1), heads_out[:, :, :, 0, :],
                                      rec1[:, b].unsqueeze(3).to_broadcast([P, TT, H1, HD1]), ALU.mult
                                      ).then_inc(dve_done, 1)
                elif what in ("y1", "y2", "y3", "y4"):
                    if what == "y1" and b == 0:
                        dve.wait_ge(tanh_done, 1)
                    residual(int(what[1]) - 1, b, bank, n + 1)
                elif what == "route":
                    dve.scalar_tensor_tensor(out=rt[:, b, :], in0=bank[0:1, 0:NH], scalar=1.0 / T,
                                             in1=W("br")[0:1, :], op0=ALU.mult, op1=ALU.add).then_inc(dve_done, 1)
                    dve.wait_ge(dve_done, n + 1)
                    link(dve.max(top[:, b, :], rt[:, b, :]))
                    link(dve.max_index(topi[:, b, :], top[:, b, :], rt[:, b, :]))
                    link(dve.tensor_scalar(negi[:, b, 0:NA], topi[:, b, 0:NA], -1.0, None, ALU.mult))
                    link(dve.max(sorti[:, b, :], negi[:, b, :]))
                    dve.tensor_scalar(heads[:, b, :], sorti[:, b, :], -1.0, None, ALU.mult).then_inc(heads_done, 1)
                elif what == "s2":
                    m = ACT_AT[step]
                    dve.wait_ge(act_full, m + 1)
                    dve.tensor_reduce(nm2[:, b, i, :], abank(m)[:].rearrange("p (t s) -> p t s", t=TT), AX.X, ALU.max,
                                      negate=True).then_inc(nm2_done, 1)
                elif what == "scale2":
                    dve.wait_ge(act_done, ACT_AT[("s2", b, i)] + 1)
                    link(dve.reciprocal(rec2[:, b, i], sum2[:, b, i]))
                    for t in range(TT):
                        ins = dve.tensor_scalar(p2[:, i, t, :], p2[:, i, t, :], rec2[:, b, i, t:t + 1], None, ALU.mult)
                    ins.then_inc(p2_scaled, 1)
                elif what == "pt2":
                    dve.tensor_copy(pT2[:, i].rearrange("p c t -> p (c t)"), bank[:]).then_inc(dve_done, 1)
                elif what == "gate":
                    dve.tensor_copy(lg[:, b].rearrange("p t e -> p (t e)"), bank[:, 0:TT * E]).then_inc(dve_done, 1)
                    dve.wait_ge(dve_done, n + 1)
                    for t in range(TT):
                        ins = dve.max(gtop[:, b, t, :], lg[:, b, t, :])
                    link(ins)
                    dve.tensor_scalar(nmax[:, b, :], gtop[:, b, :, 0], -1.0, None, ALU.mult
                                      ).then_inc(gate_max_done, 1)
                    for t in range(TT):
                        ins = dve.max_index(gidx[:, b, t, :], gtop[:, b, t, :], lg[:, b, t, :])
                    link(ins)
                    link(dve.tensor_copy(gidf[:, b], gidx[:, b, :, 0:2]))
                    iota = C("position")[:, 0:E]
                    for t in range(TT):
                        ins = dve.tensor_scalar(m1[:, b, t, :], iota, gidf[:, b, t, 0:1], None, ALU.is_equal)
                    link(ins)
                    for t in range(TT):
                        ins = dve.scalar_tensor_tensor(out=gpack[:, b, t, 2 * E:3 * E], in0=iota,
                                                       scalar=gidf[:, b, t, 1:2], in1=m1[:, b, t, :],
                                                       op0=ALU.is_equal, op1=ALU.add)
                    link(ins)
                    dve.wait_ge(gate_exp_done, b + 1)
                    link(dve.reciprocal(grec[:, b], gsum[:, b]))
                    for t in range(TT):
                        ins = dve.scalar_tensor_tensor(out=wsel[:, b, t, :], in0=gexp[:, b, t, :],
                                                       scalar=grec[:, b, t:t + 1], in1=gpack[:, b, t, 2 * E:3 * E],
                                                       op0=ALU.mult, op1=ALU.mult)
                    link(ins)
                    link(dve.tensor_copy(whi[:, b], wsel[:, b]))
                    dve.tensor_copy(gpack[:, b, :, 3 * E:4 * E], gpack[:, b, :, 2 * E:3 * E])
                    dve.tensor_copy(gpack[:, b, :, 0:E], whi[:, b].bitcast(F32))
                    dve.tensor_tensor(gpack[:, b, :, E:2 * E], wsel[:, b], whi[:, b].bitcast(F32), ALU.subtract
                                      ).then_inc(gpack_done, 1)
                elif what == "wide":
                    pair = b * E // 2 + i
                    if pair >= 2:
                        dve.wait_ge(up_read, 2 * pair - 2)
                    dve.wait_ge(act_done, ACT_AT[("norm", b, 3)] + 1)
                    dve.tensor_tensor(xw[:, i % 2], xnT[3][:, b % 2, :].unsqueeze(1).to_broadcast([P, 2, T]),
                                      bank[:].rearrange("p (e t) -> p e t", e=2), ALU.mult).then_inc(dve_done, 1)
                elif what == "down":
                    k = b * E + i
                    dve.wait_ge(act_done, ACT_AT[("up", b, i)] + 1)
                    if k >= EXPERT_BUFS:
                        dve.wait_ge(prod_read, k - EXPERT_BUFS + 1)
                    dve.scalar_tensor_tensor(out=prod[:, k % EXPERT_BUFS, :], in0=bank[:, 0:T],
                                             scalar=X("b2")[:, i:i + 1], in1=hx[:, k % EXPERT_BUFS, 1, :],
                                             op0=ALU.add, op1=ALU.mult).then_inc(dve_done, 1)
                elif what == "shared":
                    dve.wait_ge(act_done, ACT_AT[step] + 1)
                    dve.tensor_tensor(gs[:, b % 2].rearrange("p c t -> p (c t)"), bank[:],
                                      sg.rearrange("p c t -> p (c t)"), ALU.mult).then_inc(dve_done, 1)

        @block.gpsimd
        def _(pool):
            chained = [0]

            def link(ins):
                chained[0] += 1
                ins.then_inc(pool_chain, 1)
                pool.wait_ge(pool_chain, chained[0])

            link(pool.memset(half[:], -0.5))
            link(pool.memset(half8[:], -0.5))
            for step in SCHEDULE:
                what, b, i = step
                if what == "stat":
                    pool.wait_ge(stats_done, STAT_AT[step] + 1)
                    mul, add = (1.0 + EPS, EPS * EPS) if i == 2 else (1.0, EPS)
                    link(pool.tensor_scalar(veps[:, b, i, :], mv[:, b, i, :, 1], mul, add, ALU.mult, ALU.add))
                    pool.tensor_tensor(rstd[:, b, i, :], veps[:, b, i, :], half[:], ALU.pow).then_inc(rstd_done, 1)
                    if i in (1, 2):
                        pool.wait_ge(dve_done, DVE_AT[(f"y{i}", b, 0)] + 1)
                        if b >= 2:
                            pool.wait_ge(dve_done, DVE_AT[(f"y{i + 1}", b - 2, 0)] + 1)
                        pool.tensor_tensor(base[i][:, b % 2], x_of(i, b),
                                           gated_bias[:, i:i + 1, :].to_broadcast([P, TT, D]), ALU.add
                                           ).then_inc(base_done[i], 1)
                elif what == "kv":
                    pool.wait_ge(wa_in, 16)
                    pool.wait_ge(v_ones, 1)
                    pool.wait_ge(dve_done, DVE_AT[step] + 2)
                    if b >= 2:
                        pool.wait_ge(act_full, ACT_AT[("pv1", b - 2, 1)] + 1)
                    for t in range(TT):
                        ins = pool.tensor_scalar(v1[:, b % 2, t, :, 0, :], vtmp[:, t, :].rearrange("p (h d) -> p h d", h=H1),
                                                 A("mask_col")[:, b * TT + t:b * TT + t + 1], None, ALU.mult)
                    ins.then_inc(v1_done, 1)
                elif what == "gates":
                    pool.wait_ge(wb_in, 16)
                    pool.wait_ge(tanh_done, 1)
                    for k, name in enumerate(("b_out", "bo", "b_in")):
                        ins = pool.tensor_scalar(gated_bias[:, k, :], W(name), tg[:, k:k + 1], None, ALU.mult)
                    link(ins)
                elif what == "u":
                    pool.wait_ge(ssq_done, B * TT)
                    link(pool.tensor_scalar(ms[:], ssq[:], 1.0 / DC, EPS, ALU.mult, ALU.add))
                    pool.tensor_tensor(rs[:], ms[:], half8[:], ALU.pow).then_inc(rs_done, 1)
                elif what == "pv1" and i == 0:
                    pool.wait_ge(x_in[b], 16)
                    if b >= 2:
                        pool.wait_ge(dve_done, DVE_AT[("y1", b - 2, 0)] + 1)
                    pool.tensor_tensor(base[0][:, b % 2], tiles(xs, b), gated_bias[:, 0:1, :].to_broadcast([P, TT, D]),
                                       ALU.add).then_inc(base_done[0], 1)
                elif what == "down":
                    k = b * E + i
                    pool.wait_ge(dve_done, DVE_AT[step] + 1)
                    if i == 0:
                        if b >= 2:
                            pool.wait_ge(dve_done, DVE_AT[("y4", b - 2, 0)] + 1)
                        ins = pool.tensor_copy(yT[:, b % 2, :], prod[:, k % EXPERT_BUFS, :])
                    else:
                        pool.wait_ge(prod_read, k)
                        ins = pool.tensor_tensor(yT[:, b % 2, :], yT[:, b % 2, :], prod[:, k % EXPERT_BUFS, :],
                                                 ALU.add)
                    ins.then_inc(prod_read, 1)


def kernel(**inputs):
    import math

    import numpy as np
    import concourse.bacc as bacc
    from concourse.bass_utils import run_bass_kernel_spmd

    g = {k: np.asarray(v) for k, v in inputs.items()}
    f = np.float32

    def rows(v):
        return np.broadcast_to(v.reshape(1, -1), (P, v.size))

    def stacked(w, n):
        return w.reshape(n, P, -1).transpose(1, 0, 2).reshape(P, -1)

    def pack(fields, width, **parts):
        packed = np.zeros((P, width), f)
        for name, (lo, hi) in fields.items():
            packed[:, lo:hi] = parts[name]
        return packed

    order = np.arange(D).reshape(2, PAIRS, HD1).transpose(0, 2, 1).reshape(-1)
    w_src, w_out = g["L0_xattn_W_src"], g["L0_xattn_W_out"]
    mask = g["mask_BxS2_fk1"]
    pack_a = pack(PACK_A, PACK_A_W,
                  wk=stacked(w_src[:D][order].T, CC), wv=stacked(w_src[D:].T, CC),
                  wq=g["L0_xattn_W_tgt"][order].T, bq=g["L0_xattn_b_tgt"][order][:, None],
                  bk=g["L0_xattn_b_src"][:D][order][:, None], bv=rows(g["L0_xattn_b_src"][D:]),
                  mask_col=mask.reshape(B * TT, P).T)
    pack_b = pack(PACK_B, PACK_B_W,
                  wo_x=w_out[:, :D].T, wo_u=w_out[:, D:].T, b_out=rows(g["L0_xattn_b_out"]),
                  wr=g["L0_ffn_Wr"], br=rows(g["L0_ffn_br"]), wo2=stacked(g["L0_ffn_Wo"], 2), bo=rows(g["L0_ffn_bo"]),
                  w_in=g["L1_xattn_W_in"].T, b_in=rows(g["L1_xattn_b_in"]), g_res=g["L1_xattn_g_res"][:, None],
                  g_init=rows(g["L1_xattn_g_init"][:D]),
                  gates=rows(np.array([g["g_xattn"][0], g["g_ffn"][0], g["g_xattn"][1], g["g_ffn"][1]], f)))

    a = -math.expm1(-0.001)
    k = np.arange(P)
    near = k[None, :] - k[:, None]
    decay_near = np.where(near >= 0, math.exp(-0.001) * a ** np.maximum(near, 0).astype(float), 0.0)
    decay_far = math.exp(-0.001) * a ** (P + near).astype(float)
    pack_c = pack(PACK_C, PACK_C_W,
                  ident=np.eye(P), tri=(near >= 0), ones=1.0,
                  decay=np.concatenate([decay_near, decay_far], 1),
                  position=rows(np.arange(T)), row=np.stack([k + 1, k + 1 + P], 1),
                  alpha=np.where(k >= 3 * E, -1.0, 0.0)[:, None])

    def experts(w):
        return w.transpose(2, 0, 1).reshape(P, -1)

    pack_e = pack(PACK_E, PACK_E_W,
                  gate=g["L1_ffn_gate_w"].T, b1=g["L1_ffn_b1"].T, b2=g["L1_ffn_b2"].T,
                  sw1=g["L1_ffn_sw1"].T, sw2=g["L1_ffn_sw2"].T, sw3=stacked(g["L1_ffn_sw3"].T, HALVES),
                  w1=experts(g["L1_ffn_w1"]), w3=experts(g["L1_ffn_w3"]), w2=experts(g["L1_ffn_w2"]))
    sel = np.zeros((GATE_ROWS, E, P), f)
    b3 = np.zeros((GATE_ROWS, E, P), f)
    for e in range(E):
        sel[e, e] = sel[E + e, e] = 1.0
        b3[2 * E + e, e] = b3[3 * E + e, e] = g["L1_ffn_b3"][e]

    heads = [g[f"L0_ffn_W{n}"].reshape(D, NH, HD2).transpose(1, 0, 2) for n in "qkv"]
    head_biases = [g[f"L0_ffn_b{n}"].reshape(NH, HD2, 1) for n in "qkv"]
    arrays = {
        "x_tokens": g["x"], "ctx_tokens": g["ctx_2048"],
        "ctx_features": np.ascontiguousarray(g["ctx_2048"].reshape(B * T, DC).T),
        "pack_a": pack_a, "pack_b": pack_b, "pack_c": pack_c, "pack_e": pack_e,
        "mask_everywhere": np.ascontiguousarray(rows(mask)),
        "patch_lens": np.ascontiguousarray(g["mask_BxS2_if0"].reshape(B, TT, P).transpose(2, 1, 0).reshape(P, -1)),
        "head_weights": np.ascontiguousarray(np.concatenate(heads, 2)),
        "head_bias": np.ascontiguousarray(np.concatenate(head_biases, 2)),
        "gate_selectors": sel.reshape(GATE_ROWS, -1), "gate_biases": b3.reshape(GATE_ROWS, -1),
    }
    nc = bacc.Bacc("TRN2", target_bir_lowering=False, num_devices=1)
    args = [nc.dram_tensor(name, v.shape, mybir.dt.from_np(v.dtype), kind="ExternalInput").ap()
            for name, v in arrays.items()]
    out = nc.dram_tensor("out_tokens", (B, T, D), F32, kind="ExternalOutput").ap()
    flamingo(nc, *args, out)
    result = run_bass_kernel_spmd(nc, [arrays], core_ids=[0])
    return result.results[0]["out_tokens"]
```
